# Optimizing a Trainium2 kernel written in Bass

```python
import numpy as np
import jax
import jax.numpy as jnp

def _softmax(x, axis=-1):
    return jax.nn.softmax(x, axis=axis)
def _gelu(x):
    return jax.nn.gelu(x, approximate=True)
def _silu(x):
    return jax.nn.silu(x)
def _sigmoid(x):
    return jax.nn.sigmoid(x)
def _layernorm(x, axis=-1, eps=1e-5):
    m = jnp.mean(x, axis=axis, keepdims=True)
    v = jnp.var(x, axis=axis, keepdims=True)
    return (x - m) / jnp.sqrt(v + eps)
def _scatter_add(tgt, idx, src, axis=0):
    return tgt.at[idx].add(src)
def _segment_sum(src, seg, n):
    return jax.ops.segment_sum(src, seg, n)

kernel_name = 'mk_adj_preln_d1_adj_512_30dd0a'

def setup_inputs(seed: int = 0):
    np.random.seed(seed)
    _w = jnp.asarray
    def _rec_inputs():
        import jax
        import jax.numpy as jnp
        _gk = jax.random.key(seed)
        x = -0.0002928 + 1 * jax.random.normal(jax.random.fold_in(_gk, 1), (16, 1024, 512), jnp.float32)
        _a = jax.random.bernoulli(jax.random.fold_in(_gk, 2), 0.03125, (1024, 1024))
        _af = _a.astype(jnp.float32)
        adj = _af
        return x, adj
    x, adj = _rec_inputs()
    def _L0_gnn_setup():
        import jax, jax.numpy as jnp
        import numpy as np
        B, N, D, H = (4, 2048, 512, 8)
        HD = D // H
        key = jax.random.key(seed)
        ks = jax.random.split(key, 10)
        x = jax.random.normal(ks[0], (B, N, D), dtype=jnp.float32)
        adj = (jax.random.uniform(ks[1], (N, N)) < 0.1).astype(jnp.float32)
        s = 1.0 / np.sqrt(D)
        Wq = jax.random.normal(ks[2], (D, D), dtype=jnp.float32) * s
        Wk = jax.random.normal(ks[3], (D, D), dtype=jnp.float32) * s
        Wv = jax.random.normal(ks[4], (D, D), dtype=jnp.float32) * s
        Wo = jax.random.normal(ks[5], (D, D), dtype=jnp.float32) * s
        bq = jnp.zeros((D,), jnp.float32)
        bk = jnp.zeros((D,), jnp.float32)
        bv = jnp.zeros((D,), jnp.float32)
        bo = jnp.zeros((D,), jnp.float32)
        return {'x': x, 'adj': adj, 'Wq': Wq, 'bq': bq, 'Wk': Wk, 'bk': bk, 'Wv': Wv, 'bv': bv, 'Wo': Wo, 'bo': bo}
    _L0_gnn_all = _L0_gnn_setup()
    _L0_gnn_in = {k: v for k, v in _L0_gnn_all.items() if k in ('Wq', 'bq', 'Wk', 'bk', 'Wv', 'bv', 'Wo', 'bo', )}
    del _L0_gnn_all

    return {
        "x": x,
        "adj": adj,
        "L0_gnn_Wq": _L0_gnn_in["Wq"],
        "L0_gnn_bq": _L0_gnn_in["bq"],
        "L0_gnn_Wk": _L0_gnn_in["Wk"],
        "L0_gnn_bk": _L0_gnn_in["bk"],
        "L0_gnn_Wv": _L0_gnn_in["Wv"],
        "L0_gnn_bv": _L0_gnn_in["bv"],
        "L0_gnn_Wo": _L0_gnn_in["Wo"],
        "L0_gnn_bo": _L0_gnn_in["bo"],
    }

def reference(x, adj, L0_gnn_Wq, L0_gnn_bq, L0_gnn_Wk, L0_gnn_bk, L0_gnn_Wv, L0_gnn_bv, L0_gnn_Wo, L0_gnn_bo):
    import jax
    import jax.numpy as jnp
    def _L0_gnn_ref(x, adj, Wq, bq, Wk, bk, Wv, bv, Wo, bo):
        import jax, jax.numpy as jnp
        import numpy as np
        B, N, D, H = (4, 2048, 512, 8)
        HD = D // H
        b, n, d = x.shape
        q = (x @ Wq + bq).reshape(b, n, H, HD)
        k = (x @ Wk + bk).reshape(b, n, H, HD)
        v = (x @ Wv + bv).reshape(b, n, H, HD)
        scores = jnp.einsum('bqhd,bkhd->bhqk', q, k) / jnp.sqrt(jnp.float32(HD))
        scores = scores + (1.0 - adj)[None, None, :, :] * -1000000000.0
        attn = jax.nn.softmax(scores, axis=-1)
        out = jnp.einsum('bhqk,bkhd->bqhd', attn, v).reshape(b, n, d)
        return out @ Wo + bo

    h = jnp.maximum(_layernorm(x, axis=-1), 0.0)
    x = x + _L0_gnn_ref(h, adj, L0_gnn_Wq, L0_gnn_bq, L0_gnn_Wk, L0_gnn_bk, L0_gnn_Wv, L0_gnn_bv, L0_gnn_Wo, L0_gnn_bo)
    return x


_drawn_inputs = setup_inputs


def setup_inputs(seed=0):
    import zlib

    import numpy as np

    out = dict(_drawn_inputs(seed))
    spreads = {'L0_gnn_bq': (0.0, 0.8),
     'L0_gnn_bk': (0.0, 0.8),
     'L0_gnn_bv': (0.0, 0.1),
     'L0_gnn_bo': (0.0, 0.1)}
    factors = {}
    for name, (base, spread) in spreads.items():
        noise = np.random.default_rng([zlib.crc32(name.encode()), seed]).standard_normal(out[name].shape)
        drawn = base * np.exp(spread * noise) if base else spread * noise
        out[name] = jnp.asarray(drawn.astype(out[name].dtype))
    for name, factor in factors.items():
        out[name] = (out[name] * factor).astype(out[name].dtype)
    return out
```

```python
from contextlib import ExitStack

import concourse.bass as bass
from concourse import mybir

ALU = mybir.AluOpType
ACT = mybir.ActivationFunctionType
F32 = mybir.dt.float32
F32R = mybir.dt.float32r
BF16 = mybir.dt.bfloat16

P = 128
EPS = 1e-5
NEG = 1e9
BANK = 512
MX_OF_STEP = [0, 0, 3, 3, 3, 3, 4, 0]
MROW_A_STEP, MROW_B_STEP = 5, 7
OUT_OF_STEP = [0, 0, 0, 2, 2, 1, 2, 1]


class Shapes:
    def __init__(self, x, heads):
        self.B, self.N, self.D = x.shape
        self.H = heads
        self.HD = self.D // heads
        self.C = self.D // P
        self.T = self.N // P
        self.PAIRS = heads // 2
        self.HALVES = self.N // BANK
        assert self.HD == 64 and self.N == 1024 and self.D == BANK and self.PAIRS == self.C


def after(eng, sem, count):
    if isinstance(count, int) and count <= 0:
        return
    eng.wait_ge(sem, count)


def wait_apart(eng, sem, count, passed):
    eng.wait_ge(sem, count)
    eng.sem_inc(passed, 1)


def halves(n=2):
    return [(h, slice(h * BANK, (h + 1) * BANK)) for h in range(n)]


def project_stage(nc, sh, ctx_outer, io, scratch, keep):
    x, adj, Wq, bq, Wk, bk, Wv, bv, Wo, bo = io
    qk_d, v_d = scratch
    mask, maskT, Wo_hi, Wo_lo, bo_bc, ident, identb = keep
    B, C, T, PAIRS = sh.B, sh.C, sh.T, sh.PAIRS
    J = 2 * PAIRS
    with ExitStack() as ctx:
        def sb(name, shape, dt):
            return ctx.enter_context(nc.sbuf_tensor(name, shape, dt))

        def sem(name):
            return ctx.enter_context(nc.semaphore(name))

        W_hi = [sb(f"w{n}_hi", [P, C, sh.D], F32R) for n in "qkv"] + [Wo_hi]
        W_lo = [sb(f"w{n}_lo", [P, C, sh.D], F32R) for n in "qkv"] + [Wo_lo]
        xs = sb("xs", [P, T, sh.D], F32)
        hT_hi = sb("hT_hi", [P, C, sh.N], F32R)
        hT_lo = sb("hT_lo", [P, C, sh.N], F32R)
        hi_out = sb("hi_out", [P, 2, sh.N], F32R)
        lo_out = sb("lo_out", [P, 2, sh.N], F32R)
        v_out = sb("v_out", [P, PAIRS, T, P], F32)
        bv_bc = sb("bv_bc", [P, sh.D], F32)
        bqk = sb("bqk", [P, PAIRS, 2], F32)
        stats = sb("stats", [P, T, 6], F32)
        mv = sb("mv", [P, T, 2], F32)
        ve = sb("ve", [P, T], F32)
        rv = sb("rv", [P, T], F32)
        y0 = sb("y0", [P, T], F32)
        t1 = sb("t1", [P, T], F32)
        t2 = sb("t2", [P, T], F32)
        t3 = sb("t3", [P, T], F32)
        rstd = sb("rstd", [P, T], F32)
        nmr = sb("nmr", [P, T], F32)
        tp = ctx.enter_context(nc.psum_tensor("tp", [P, 2, BANK], F32))
        qk_ps = ctx.enter_context(nc.psum_tensor("qk_ps", [P, 2, sh.N], F32))
        v_ps = ctx.enter_context(nc.psum_tensor("v_ps", [P, 2, BANK], F32))

        w_loaded = [sem(f"w_loaded{i}") for i in range(4)]
        bias_loaded = sem("bias_loaded")
        adj_loaded = sem("adj_loaded")
        x_loaded = sem("x_loaded")
        zeroed = sem("zeroed")
        ident_made = sem("ident_made")
        identb_made = sem("identb_made")
        bias_scaled = sem("bias_scaled")
        w_hi_made = sem("w_hi_made")
        w_lo_made = sem("w_lo_made")
        adj_turned = sem("adj_turned")
        maskT_made = sem("maskT_made")
        mask_made = sem("mask_made")
        ln_steps = sem("ln_steps")
        sqrt_made = sem("sqrt_made")
        stats_passed = sem("stats_passed")
        h_made = sem("h_made")
        h_turned = sem("h_turned")
        hT_hi_made = sem("hT_hi_made")
        hT_lo_made = sem("hT_lo_made")
        qk_ready = sem("qk_ready")
        qk_hi_made = sem("qk_hi_made")
        qk_lo_made = sem("qk_lo_made")
        v_ready = sem("v_ready")
        v_made = sem("v_made")
        qk_stored = [sem(f"qk_stored{i}") for i in range(2)]
        v_stored = sem("v_stored")

        v_flat = v_out[:, :, :, :].rearrange("p a t n -> p (a t n)").rearrange("p (w c n) -> p w c n", w=2, c=C)
        W_raw = [xs[:, 0:C, :], xs[:, C:2 * C, :], v_flat[:, 0], v_flat[:, 1]]
        W_scale = [1.0 / 8.0, 1.0, 1.0, 1.0]
        LN_OPS = 2 * T + 7

        block = ctx.enter_context(nc.Block())

        @block.sync
        def _(sp):
            for i, w in enumerate((Wq, Wk, Wv, Wo)):
                sp.dma_start(W_raw[i], w.rearrange("(c p) n -> p c n", p=P)).then_inc(w_loaded[i], 16)
                if i == 1:
                    sp.dma_start(mask[:, :, :], adj.rearrange("(t p) n -> p t n", p=P)).then_inc(adj_loaded, 16)
            with nc.allow_non_contiguous_dma(reason="two vectors of 512, once"):
                sp.dma_start(bqk[:, :, 0], bq.rearrange("(c p) -> p c", p=P)).then_inc(bias_loaded, 16)
                sp.dma_start(bqk[:, :, 1], bk.rearrange("(c p) -> p c", p=P)).then_inc(bias_loaded, 16)
            sp.dma_start(bv_bc[:, :], bv.rearrange("(a n) -> a n", a=1).partition_broadcast(P)).then_inc(bias_loaded, 16)
            sp.dma_start(bo_bc[:, :], bo.rearrange("(a n) -> a n", a=1).partition_broadcast(P)).then_inc(bias_loaded, 16)
            sp.wait_ge(w_lo_made, 2)
            sp.dma_start(xs[:, :, :], x[0].rearrange("(t p) n -> p t n", p=P)).then_inc(x_loaded, 16)

            def step(b, last):
                if not last:
                    sp.wait_ge(h_turned, b * T + T)
                    sp.dma_start(xs[:, :, :], x[b + 1].rearrange("(t p) n -> p t n", p=P)).then_inc(x_loaded, 16)
                for j in range(J):
                    sp.wait_ge(qk_hi_made, b * J + (j + 1))
                    sp.dma_start(qk_d[b, j // 2, 2 * (j % 2)], hi_out[:, j % 2, :].bitcast(F32)).then_inc(qk_stored[j % 2], 16)
                    sp.wait_ge(qk_lo_made, b * J + (j + 1))
                    sp.dma_start(qk_d[b, j // 2, 2 * (j % 2) + 1], lo_out[:, j % 2, :].bitcast(F32)).then_inc(qk_stored[j % 2], 16)
                sp.wait_ge(v_made, b * T + T)
                sp.dma_start(v_d[b].rearrange("a p n -> p a n"),
                             v_out[:, :, :, :].rearrange("p a t n -> p a (t n)")).then_inc(v_stored, 16)

            with sp.Fori(0, B - 1) as b:
                step(b, False)
            step(B - 1, True)
            for i in range(2):
                sp.wait_ge(qk_stored[i], 32 * (J // 2) * B)
            sp.wait_ge(v_stored, 16 * B)

        @block.gpsimd
        def _(pool):
            nc.gpsimd.memset(ident[:, :], 0.0).then_inc(zeroed, 1)
            pool.wait_ge(zeroed, 1)
            nc.gpsimd.affine_select(out=ident[:, :], in_=ident[:, :], compare_op=ALU.not_equal, fill=1.0, base=0,
                                    pattern=[[-1, P]], channel_multiplier=1).then_inc(ident_made, 1)

        @block.scalar
        def _(act):
            for i in range(4):
                act.wait_ge(w_loaded[i], 16)
                nc.scalar.mul(W_hi[i][:, :, :], W_raw[i], W_scale[i]).then_inc(w_hi_made, 1)

            def relu_ln(b):
                act.wait_ge(ln_steps, b * LN_OPS + 2 * T + 2)
                nc.scalar.activation(y0[:, :], rv[:, :], ACT.Sqrt).then_inc(sqrt_made, 1)
                act.wait_ge(ln_steps, b * LN_OPS + LN_OPS)
                for t in range(T):
                    nc.scalar.activation(xs[:, t, :], xs[:, t, :], ACT.Relu, bias=nmr[:, t:t + 1],
                                         scale=rstd[:, t:t + 1]).then_inc(h_made, 1)

            def step(b, last):
                for t in range(T):
                    act.wait_ge(h_turned, b * T + (t + 1))
                    nc.scalar.copy(hT_hi[:, :, t * P:(t + 1) * P],
                                   tp[:, t % 2, :].rearrange("p (c n) -> p c n", c=C)).then_inc(hT_hi_made, 1)
                for j in range(J):
                    act.wait_ge(qk_ready, b * J + (j + 1))
                    after(act, qk_stored[j % 2], b * (32 * (J // 2)) + 32 * (j // 2))
                    nc.scalar.activation(hi_out[:, j % 2, :], qk_ps[:, j % 2, :], ACT.Identity,
                                         bias=bqk[:, j // 2, j % 2:j % 2 + 1]).then_inc(qk_hi_made, 1)
                    if j == 3 and not last:
                        relu_ln(b + 1)

            act.wait_ge(bias_scaled, 1)
            relu_ln(0)
            first_then_loop(act, B, step)

        @block.vector
        def _(dve):
            for i in range(4):
                dve.wait_ge(w_hi_made, i + 1)
                nc.vector.scalar_tensor_tensor(out=W_lo[i][:, :, :].rearrange("p c n -> p (c n)"),
                                               in0=W_raw[i].rearrange("p c n -> p (c n)"), scalar=W_scale[i],
                                               in1=W_hi[i][:, :, :].bitcast(F32).rearrange("p c n -> p (c n)"),
                                               op0=ALU.mult, op1=ALU.subtract).then_inc(w_lo_made, 1)
            dve.wait_ge(bias_loaded, 64)
            nc.vector.tensor_scalar(bqk[:, :, 0], bqk[:, :, 0], W_scale[0], None, ALU.mult).then_inc(bias_scaled, 1)
            dve.wait_ge(ident_made, 1)
            nc.vector.tensor_copy(identb[:, :], ident[:, :]).then_inc(identb_made, 1)

            def layer_norm(b):
                at = b * LN_OPS
                dve.wait_ge(x_loaded, b * 16 + 16)
                for t in range(T):
                    nc.vector.bn_stats(stats[:, t, :], xs[:, t, :]).then_inc(ln_steps, 1)
                wait_apart(dve, ln_steps, at + T, stats_passed)
                for t in range(T):
                    nc.vector.bn_aggr(mv[:, t, :], stats[:, t, :]).then_inc(ln_steps, 1)
                dve.wait_ge(ln_steps, at + 2 * T)
                nc.vector.tensor_scalar(ve[:, :], mv[:, :, 1], EPS, None, ALU.add).then_inc(ln_steps, 1)
                dve.wait_ge(ln_steps, at + 2 * T + 1)
                nc.vector.reciprocal(rv[:, :], ve[:, :]).then_inc(ln_steps, 1)
                dve.wait_ge(sqrt_made, b + 1)
                nc.vector.tensor_tensor(t1[:, :], y0[:, :], y0[:, :], ALU.mult).then_inc(ln_steps, 1)
                dve.wait_ge(ln_steps, at + 2 * T + 3)
                nc.vector.tensor_tensor(t2[:, :], t1[:, :], ve[:, :], ALU.mult).then_inc(ln_steps, 1)
                dve.wait_ge(ln_steps, at + 2 * T + 4)
                nc.vector.tensor_scalar(t3[:, :], t2[:, :], -0.5, 1.5, ALU.mult, ALU.add).then_inc(ln_steps, 1)
                dve.wait_ge(ln_steps, at + 2 * T + 5)
                nc.vector.tensor_tensor(rstd[:, :], y0[:, :], t3[:, :], ALU.mult).then_inc(ln_steps, 1)
                dve.wait_ge(ln_steps, at + 2 * T + 6)
                nc.vector.scalar_tensor_tensor(out=nmr[:, :], in0=mv[:, :, 0], scalar=-1.0, in1=rstd[:, :],
                                               op0=ALU.mult, op1=ALU.mult).then_inc(ln_steps, 1)

            layer_norm(0)
            for t in range(T):
                for h, cols in halves():
                    g = 2 * t + h
                    dve.wait_ge(adj_turned, g + 1)
                    nc.vector.tensor_scalar(maskT[:, t, cols], v_ps[:, g % 2, :], -1.0, None,
                                            ALU.add).then_inc(maskT_made, 1)
            for t in range(T):
                nc.vector.tensor_scalar(mask[:, t, :], mask[:, t, :], -1.0, NEG, ALU.add,
                                        ALU.mult).then_inc(mask_made, 1)

            def step(b, last):
                for t in range(T):
                    dve.wait_ge(hT_hi_made, b * T + (t + 1))
                    cols = slice(t * P, (t + 1) * P)
                    nc.vector.tensor_tensor(hT_lo[:, :, cols], tp[:, t % 2, :].rearrange("p (c n) -> p c n", c=C),
                                            hT_hi[:, :, cols].bitcast(F32), ALU.subtract).then_inc(hT_lo_made, 1)
                for j in range(J):
                    dve.wait_ge(qk_hi_made, b * J + (j + 1))
                    nc.vector.scalar_tensor_tensor(out=lo_out[:, j % 2, :], in0=qk_ps[:, j % 2, :],
                                                   scalar=bqk[:, j // 2, j % 2:j % 2 + 1],
                                                   in1=hi_out[:, j % 2, :].bitcast(F32), op0=ALU.add,
                                                   op1=ALU.subtract).then_inc(qk_lo_made, 1)
                    if j == 2 and not last:
                        layer_norm(b + 1)
                after(dve, v_stored, b * 16)
                for t in range(T):
                    dve.wait_ge(v_ready, b * T + (t + 1))
                    nc.vector.tensor_tensor(v_out[:, :, t, :], v_ps[:, t % 2, :].rearrange("p (a n) -> p a n", a=PAIRS),
                                            bv_bc[:, :].rearrange("p (a n) -> p a n", a=PAIRS),
                                            ALU.add).then_inc(v_made, 1)

            first_then_loop(dve, B, step)

        @block.tensor
        def _(pe):
            pe.wait_ge(ident_made, 1)
            pe.wait_ge(adj_loaded, 16)
            for t in range(T):
                for h in range(2):
                    g = 2 * t + h
                    after(pe, maskT_made, g - 1)
                    for i in range(4):
                        qt = 4 * h + i
                        mm = pe.transpose(v_ps[:, g % 2, i * P:(i + 1) * P], mask[:, qt, t * P:(t + 1) * P], ident[:, :])
                    mm.then_inc(adj_turned, 1)
            pe.wait_ge(w_lo_made, 4)
            pe.wait_ge(maskT_made, 2 * T)

            def three_passes(out, lhs, rhs, n):
                for c in range(n):
                    for k, (l, r) in enumerate(((0, 0), (0, 1), (1, 0))):
                        mm = pe.matmul(out, lhs(l, c), rhs(r, c), start=(c == 0 and k == 0), stop=(c == n - 1 and k == 2))
                return mm

            hT = (hT_hi, hT_lo)

            def step(b, last):
                for t in range(T):
                    pe.wait_ge(h_made, b * T + (t + 1))
                    after(pe, hT_lo_made, b * T + (t - 1))
                    for c in range(C):
                        mm = pe.transpose(tp[:, t % 2, c * P:(c + 1) * P], xs[:, t, c * P:(c + 1) * P], ident[:, :])
                    mm.then_inc(h_turned, 1)
                for j in range(J):
                    w = (W_hi[j % 2], W_lo[j % 2])
                    after(pe, qk_lo_made, b * J + (j - 1))
                    for h, cols in halves():
                        if j == 0:
                            pe.wait_ge(hT_lo_made, b * T + 4 * (h + 1))
                        mm = three_passes(qk_ps[:, j % 2, cols],
                                          lambda l, c: w[l][:, c, (j // 2) * P:(j // 2 + 1) * P],
                                          lambda r, c: hT[r][:, c, cols], C)
                    mm.then_inc(qk_ready, 1)
                for t in range(T):
                    after(pe, v_made, b * T + (t - 1))
                    mm = three_passes(v_ps[:, t % 2, :], lambda l, c: hT[l][:, c, t * P:(t + 1) * P],
                                      lambda r, c: (W_hi[2], W_lo[2])[r][:, c, :], C)
                    mm.then_inc(v_ready, 1)

            first_then_loop(pe, B, step)


def first_then_loop(eng, count, step):
    step(0, False)
    with eng.Fori(1, count - 1) as b:
        step(b, False)
    step(count - 1, True)


def attend_stage(nc, sh, io, scratch, keep, out):
    x = io[0]
    qk_d, v_d = scratch
    mask, maskT, Wo_hi, Wo_lo, bo_bc, ident, identb = keep
    B, N, D, T, PAIRS, HD = sh.B, sh.N, sh.D, sh.T, sh.PAIRS, sh.HD
    U = 2 * T
    MROWS = 3
    KB_ROWS = HD + MROWS
    ADDS = 2 * (T - 1)
    RING = 2
    with ExitStack() as ctx:
        def sb(name, shape, dt):
            return ctx.enter_context(nc.sbuf_tensor(name, shape, dt))

        def sem(name):
            return ctx.enter_context(nc.semaphore(name))

        k_hl = sb("k_hl", [P, 2, 2, N], F32R)
        q_hh = sb("q_hh", [P, 2, 2, N], F32R)
        k_h1 = sb("k_h1", [P, 2, 2, N], F32R)
        q_lm = sb("q_lm", [P, 2, 2, N], F32R)
        v_sb = sb("v_sb", [P, 2, T, P], F32)
        probs = sb("probs", [P, 2, 2, N], F32)
        acc = sb("acc", [P, 2, N], F32)
        o_sb = sb("o_sb", [P, N], F32)
        oT_hi = sb("oT_hi", [P, PAIRS, N], F32R)
        oT_lo = sb("oT_lo", [P, PAIRS, N], F32R)
        xy = sb("xy", [P, RING, D], F32)
        ones = sb("ones", [P, HD], F32)
        qmax = sb("qmax", [P, 2, T], F32)
        rest = sb("rest", [P, 2, T], F32)
        pieces = sb("pieces", [P, 2, T, KB_ROWS + 1], BF16)

        def pb(name, cols):
            return ctx.enter_context(nc.psum_tensor(name, [P, cols], F32))

        mx_ps = pb("mx_ps", N)
        st_ps = pb("st_ps", N)
        o_ps = pb("o_ps", N)
        misc = pb("misc", N)

        qk_loaded = [sem(f"qk_loaded{i}") for i in range(2)]
        qk2_loaded = [sem(f"qk2_loaded{i}") for i in range(2)]
        v_loaded = [sem(f"v_loaded{i}") for i in range(2)]
        x_loaded = [sem(f"x2_loaded{i}") for i in range(RING)]
        y_stored = [sem(f"y_stored{i}") for i in range(RING)]
        consts = sem("consts")
        mx_ready = sem("mx_ready")
        mx_taken = sem("mx_taken")
        mx_passed = sem("mx_passed")
        stores_passed = sem("stores_passed")
        m_steps = sem("m_steps")
        mrow_ready = sem("mrow_ready")
        mrow_kept = sem("mrow_kept")
        st_ready = sem("st_ready")
        st_masked = sem("st_masked")
        exp_done = sem("exp_done")
        pv_done = sem("pv_done")
        o_copied = sem("o_copied")
        added = sem("added")
        sum_ready = sem("sum_ready")
        log_taken = sem("log_taken")
        recip_ready = sem("recip_ready")
        o_normed = sem("o_normed")
        oT_hi_made = sem("oT_hi_made")
        oT_lo_made = sem("oT_lo_made")
        y_ready = sem("y_ready")
        xbo_made = sem("xbo_made")
        y_made = sem("y_made")

        block = ctx.enter_context(nc.Block())
        NS = B * PAIRS
        LOOP = 4
        before = [sum(MX_OF_STEP[:s]) for s in range(T)]
        outs_before = [sum(OUT_OF_STEP[:s]) for s in range(T)]

        def is_last(n):
            return isinstance(n, int) and n == NS - 1

        def is_first(n):
            return isinstance(n, int) and n == 0

        @block.sync
        def _(sp):
            def load(b, pair, par, n, v_too=True):
                src = lambda i: qk_d[b, pair, i].rearrange("(h p) n -> p h n", h=2)
                lo, hi = slice(0, HD), slice(HD, P)
                QHI, QLO, KHI, KLO = range(4)
                for dst, rows, s in ((q_hh, lo, QHI), (k_hl, lo, KHI), (q_hh, hi, QHI), (k_hl, hi, KLO)):
                    sp.dma_start(dst[rows, par].bitcast(F32), src(s)).then_inc(qk_loaded[par], 16)
                for dst, s in ((k_h1, KHI), (q_lm, QLO)):
                    sp.dma_start(dst[lo, par].bitcast(F32), src(s)).then_inc(qk2_loaded[par], 16)
                if v_too:
                    after(sp, pv_done, n * T - T)
                    sp.dma_start(v_sb[:, par].rearrange("p t n -> p (t n)"), v_d[b, pair]).then_inc(v_loaded[par], 16)

            def outs(b):
                for i in range(T + RING):
                    if i < T:
                        if i >= RING:
                            sp.wait_ge(y_made, b * T + (i - RING + 1))
                            sp.dma_start(out[b, (i - RING) * P:(i - RING + 1) * P, :], xy[:, i % RING, :]).then_inc(y_stored[i % RING], 16)
                            sp.wait_ge(y_stored[i % RING], b * (16 * T // RING) + 16 * (i // RING))
                        sp.dma_start(xy[:, i % RING, :], x[b, i * P:(i + 1) * P, :]).then_inc(x_loaded[i % RING], 16)
                    else:
                        sp.wait_ge(y_made, b * T + (i - RING + 1))
                        sp.dma_start(out[b, (i - RING) * P:(i - RING + 1) * P, :], xy[:, i % RING, :]).then_inc(y_stored[i % RING], 16)
                for i in range(RING):
                    wait_apart(sp, y_stored[i], (b + 1) * (16 * T // RING), stores_passed)

            load(0, 0, 0, 0)

            def slot(n, p, b_next, b_prev):
                if not is_last(n):
                    after(sp, st_ready, n * U)
                    load(b_next, (p + 1) % PAIRS, (p + 1) % 2, n + 1)
                if p == 0 and not is_first(n):
                    outs(b_prev)

            slot(0, 0, 0, 0)
            with sp.Fori(0, B - 1) as b:
                for i in range(1, LOOP + 1):
                    slot(b * PAIRS + i, i % PAIRS, b if i < 3 else b + 1, b)
            for n in range(NS - 3, NS):
                slot(n, n % PAIRS, B - 1, B - 1)
            outs(B - 1)

        @block.gpsimd
        def _(pool):
            nc.gpsimd.memset(pieces[:, :, :, :], 0.0).then_inc(consts, 1)
            nc.gpsimd.memset(ones[:, :], 1.0).then_inc(consts, 1)
            pool.wait_ge(consts, 2)
            nc.gpsimd.memset(k_h1[HD:P, :, :, :].bitcast(F32), 1.0).then_inc(consts, 1)
            pool.wait_ge(consts, 3)

            def low_part(n, pair):
                pool.wait_ge(oT_hi_made, n + 1)
                nc.gpsimd.tensor_tensor(oT_lo[:, pair, :], o_sb[:, :], oT_hi[:, pair, :].bitcast(F32),
                                        ALU.subtract).then_inc(oT_lo_made, 1)

            def add_bo(b, i):
                pool.wait_ge(x_loaded[i % RING], b * (16 * T // RING) + 16 * (i // RING + 1))
                nc.gpsimd.tensor_tensor(xy[:, i % RING, :], xy[:, i % RING, :], bo_bc[:, :],
                                        ALU.add).then_inc(xbo_made, 1)

            def slot(n, p, b_prev):
                for t in range(1, T):
                    if p == 0 and not is_first(n):
                        for i in range(outs_before[t], outs_before[t] + OUT_OF_STEP[t]):
                            add_bo(b_prev, i)
                    for hd in range(2):
                        pool.wait_ge(exp_done, n * U + (2 * t + hd + 1))
                        if t == 1:
                            after(pool, sum_ready, n)
                            ins = (probs[:, 0, hd, :], probs[:, 1, hd, :])
                        else:
                            pool.wait_ge(added, n * ADDS + (2 * (t - 2) + hd + 1))
                            ins = (acc[:, hd, :], probs[:, t % 2, hd, :])
                        nc.gpsimd.tensor_tensor(acc[:, hd, :], ins[0], ins[1], ALU.add).then_inc(added, 1)
                    if t == 3 and not is_first(n):
                        low_part(n - 1, (p - 1) % PAIRS)
            slot(0, 0, 0)
            with pool.Fori(0, B - 1) as b:
                for i in range(1, LOOP + 1):
                    slot(b * PAIRS + i, i % PAIRS, b)
            for n in range(NS - 3, NS):
                slot(n, n % PAIRS, B - 1)
            low_part(NS - 1, PAIRS - 1)
            for i in range(T):
                add_bo(B - 1, i)

        @block.scalar
        def _(act):
            def exp(n, s, hd):
                act.wait_ge(st_masked, n * U + (2 * s + hd + 1))
                nc.scalar.activation(probs[:, s % 2, hd, :], probs[:, s % 2, hd, :], ACT.Exp).then_inc(exp_done, 1)

            def keep_mrows(n, par, hd):
                act.wait_ge(mrow_ready, n * 2 + (hd + 1))
                nc.scalar.copy(q_lm[HD:KB_ROWS, par, hd, :], misc[HD:KB_ROWS, :]).then_inc(mrow_kept, 1)

            def copy_o(n):
                act.wait_ge(pv_done, n * T + T)
                nc.scalar.copy(o_sb[:, :], o_ps[:, :]).then_inc(o_copied, 1)

            def recip(n):
                act.wait_ge(sum_ready, n + 1)
                nc.scalar.activation(misc[:, :], misc[:, :], ACT.Ln).then_inc(log_taken, 1)
                act.wait_ge(log_taken, n + 1)
                nc.scalar.activation(misc[:, :], misc[:, :], ACT.Exp, scale=-1.0).then_inc(recip_ready, 1)

            def high_part(n, pair):
                act.wait_ge(o_normed, n + 1)
                nc.scalar.copy(oT_hi[:, pair, :], o_sb[:, :]).then_inc(oT_hi_made, 1)

            def slot(n, p, b_prev):
                for s in range(T):
                    exp(n, s, 0)
                    if s == MROW_B_STEP and not is_last(n):
                        keep_mrows(n + 1, (p + 1) % 2, 1)
                    exp(n, s, 1)
                    if not is_first(n):
                        if s == 0:
                            copy_o(n - 1)
                        if s == 1:
                            recip(n - 1)
                        if s == 2:
                            high_part(n - 1, (p - 1) % PAIRS)
                    if s == MROW_A_STEP and not is_last(n):
                        keep_mrows(n + 1, (p + 1) % 2, 0)

            keep_mrows(0, 0, 0)
            keep_mrows(0, 0, 1)
            slot(0, 0, 0)
            with act.Fori(0, B - 1) as b:
                for i in range(1, LOOP + 1):
                    slot(b * PAIRS + i, i % PAIRS, b)
            for n in range(NS - 3, NS):
                slot(n, n % PAIRS, B - 1)
            copy_o(NS - 1)
            recip(NS - 1)
            high_part(NS - 1, PAIRS - 1)

        @block.vector
        def _(dve):
            def mask_scores(n, s, hd):
                dve.wait_ge(st_ready, n * U + (2 * s + hd + 1))
                after(dve, pv_done, n * T + (s - 1))
                t = s - 2 if s >= 2 else T + s - 2
                t = max(t, 1)
                after(dve, added, n * ADDS + (2 * (t - 1) + hd + 1 - (ADDS if s < 2 else 0)))
                nc.vector.scalar_tensor_tensor(out=probs[:, s % 2, hd, :], in0=maskT[:, s, :], scalar=NEG,
                                               in1=st_ps[:, :], op0=ALU.mult, op1=ALU.add).then_inc(st_masked, 1)

            def take_max(n, j):
                wait_apart(dve, mx_ready, n * U + (j + 1), mx_passed)
                nc.vector.tensor_tensor_reduce(mx_ps[:, :], mx_ps[:, :], mask[:, j % T, :], 1.0, -3.0e38, ALU.add,
                                               ALU.max, qmax[:, j // T, j % T:j % T + 1]).then_inc(mx_taken, 1)

            def split_max(n, hd):
                piece = [pieces[:, hd, :, HD + i] for i in range(MROWS)]
                at = n * 8 + 4 * hd
                dve.wait_ge(mx_taken, n * U + T * (hd + 1))
                after(dve, mrow_ready, n * 2 + (hd - 1))
                nc.vector.tensor_scalar(piece[0], qmax[:, hd, :], -1.0, None, ALU.mult).then_inc(m_steps, 1)
                dve.wait_ge(m_steps, at + 1)
                nc.vector.scalar_tensor_tensor(out=rest[:, hd, :], in0=qmax[:, hd, :], scalar=-1.0, in1=piece[0],
                                               op0=ALU.mult, op1=ALU.subtract).then_inc(m_steps, 1)
                dve.wait_ge(m_steps, at + 2)
                nc.vector.tensor_copy(piece[1], rest[:, hd, :]).then_inc(m_steps, 1)
                dve.wait_ge(m_steps, at + 3)
                nc.vector.tensor_tensor(piece[2], rest[:, hd, :], piece[1], ALU.subtract).then_inc(m_steps, 1)

            def norm(n):
                dve.wait_ge(recip_ready, n + 1)
                nc.vector.tensor_tensor(o_sb[:, :], o_sb[:, :], misc[:, :], ALU.mult).then_inc(o_normed, 1)

            def add_out(b, i):
                dve.wait_ge(y_ready, b * T + (i + 1))
                dve.wait_ge(xbo_made, b * T + (i + 1))
                nc.vector.tensor_tensor(xy[:, i % RING, :], misc[:, (i % 2) * BANK:(i % 2 + 1) * BANK],
                                        xy[:, i % RING, :], ALU.add).then_inc(y_made, 1)

            def slot(n, p, b_prev):
                for s in range(T):
                    mask_scores(n, s, 0)
                    js = [] if is_last(n) else list(range(before[s], before[s] + MX_OF_STEP[s]))
                    for j in js[:1]:
                        take_max(n + 1, j)
                    mask_scores(n, s, 1)
                    for j in js[1:]:
                        take_max(n + 1, j)
                        if j == T:
                            split_max(n + 1, 0)
                    if js and js[-1] == U - 1:
                        split_max(n + 1, 1)
                    if s == 2 and not is_first(n):
                        norm(n - 1)
                    if p == 0 and not is_first(n):
                        for i in range(outs_before[s], outs_before[s] + OUT_OF_STEP[s]):
                            add_out(b_prev, i)

            dve.wait_ge(consts, 3)
            for j in range(U):
                take_max(0, j)
                if j % T == T - 1:
                    split_max(0, j // T)
            slot(0, 0, 0)
            with dve.Fori(0, B - 1) as b:
                for i in range(1, LOOP + 1):
                    slot(b * PAIRS + i, i % PAIRS, b)
            for n in range(NS - 3, NS):
                slot(n, n % PAIRS, B - 1)
            norm(NS - 1)
            for i in range(T):
                add_out(B - 1, i)

        @block.tensor
        def _(pe):
            def query_scores(n, j, par, loads):
                hd, qt = j // T, j % T
                if j == 0:
                    pe.wait_ge(qk_loaded[par], loads * 64)
                after(pe, mx_taken, n * U + j)
                for h, cols in halves():
                    mm = pe.matmul(mx_ps[:, cols], q_hh[:, par, hd, qt * P:(qt + 1) * P], k_hl[:, par, hd, cols],
                                   start=True, stop=True)
                mm.then_inc(mx_ready, 1)

            def max_rows(n, hd):
                pe.wait_ge(m_steps, n * 8 + 4 * (hd + 1))
                for qt in range(T):
                    mm = pe.matmul(misc[0:KB_ROWS, qt * P:(qt + 1) * P], pieces[:, hd, qt, 0:KB_ROWS], identb[:, :],
                                   start=True, stop=True)
                mm.then_inc(mrow_ready, 1)

            def key_scores(n, s, hd, par, loads):
                if s == 0:
                    pe.wait_ge(mrow_kept, n * 2 + (hd + 1))
                    if hd == 0:
                        pe.wait_ge(qk2_loaded[par], loads * 32)
                after(pe, st_masked, n * U + (2 * s + hd))
                keys = slice(s * P, (s + 1) * P)
                for h, cols in halves():
                    pe.matmul(st_ps[:, cols], k_hl[:, par, hd, keys], q_hh[:, par, hd, cols], start=True, stop=False)
                for h, cols in halves():
                    mm = pe.matmul(st_ps[:, cols], k_h1[0:KB_ROWS, par, hd, keys], q_lm[0:KB_ROWS, par, hd, cols],
                                   start=False, stop=True)
                mm.then_inc(st_ready, 1)

            def weigh(n, s, par, loads):
                if s == 0:
                    pe.wait_ge(v_loaded[par], loads * 16)
                    after(pe, o_copied, n)
                pe.wait_ge(exp_done, n * U + (2 * s + 2))
                for h, cols in halves():
                    for hd in range(2):
                        rows = slice(hd * HD, (hd + 1) * HD)
                        mm = pe.matmul(o_ps[rows, cols], v_sb[:, par, s, rows], probs[:, s % 2, hd, cols],
                                       start=(s == 0), stop=(s == T - 1))
                mm.then_inc(pv_done, 1)

            def sums(n):
                pe.wait_ge(added, n * ADDS + ADDS)
                for h, cols in halves():
                    for hd in range(2):
                        rows = slice(hd * HD, (hd + 1) * HD)
                        mm = pe.matmul(misc[rows, cols], ones[:, :], acc[:, hd, cols], start=True, stop=True)
                mm.then_inc(sum_ready, 1)

            def project_out(b, i):
                toks = slice(i * P, (i + 1) * P)
                o = misc[:, (i % 2) * BANK:(i % 2 + 1) * BANK]
                if i == 0:
                    pe.wait_ge(oT_lo_made, b * PAIRS + PAIRS)
                if i >= 2:
                    pe.wait_ge(y_made, b * T + (i - 1))
                for c in range(PAIRS):
                    for k, (l, r) in enumerate(((oT_hi, Wo_hi), (oT_hi, Wo_lo), (oT_lo, Wo_hi))):
                        mm = pe.matmul(o, l[:, c, toks], r[:, c, :], start=(c == 0 and k == 0),
                                       stop=(c == PAIRS - 1 and k == 2))
                mm.then_inc(y_ready, 1)

            def slot(n, p, half, b_prev):
                par = p % 2
                nxt = (p + 1) % 2
                loads = half + 1
                loads_next = loads + 1 if par == 1 else loads
                prev_loads = loads if par == 1 else half
                outs = p == 0 and not is_first(n)
                for s in range(T):
                    js = [] if is_last(n) else list(range(before[s], before[s] + MX_OF_STEP[s]))
                    key_scores(n, s, 0, par, loads)
                    for j in js[:1]:
                        query_scores(n + 1, j, nxt, loads_next)
                    key_scores(n, s, 1, par, loads)
                    for j in js[1:2]:
                        query_scores(n + 1, j, nxt, loads_next)
                    if s == 0:
                        if not is_first(n):
                            weigh(n - 1, T - 1, nxt, prev_loads)
                    else:
                        weigh(n, s - 1, par, loads)
                    for j in js[2:]:
                        query_scores(n + 1, j, nxt, loads_next)
                    if s == 1 and not is_first(n):
                        sums(n - 1)
                    if outs and OUT_OF_STEP[s]:
                        pe.wait_ge(o_normed, n)
                        if s > MROW_A_STEP:
                            pe.wait_ge(mrow_kept, n * 2 + 3)
                        for i in range(outs_before[s], outs_before[s] + OUT_OF_STEP[s]):
                            project_out(b_prev, i)
                    if not is_last(n) and s in (MROW_A_STEP, MROW_B_STEP):
                        after(pe, o_normed, n)
                        if s == MROW_B_STEP:
                            pe.wait_ge(mrow_kept, n * 2 + 3)
                        if outs:
                            pe.wait_ge(y_made, b_prev * T + outs_before[s] + OUT_OF_STEP[s])
                        max_rows(n + 1, 0 if s == MROW_A_STEP else 1)

            for j in range(U):
                query_scores(0, j, 0, 1)
            pe.wait_ge(consts, 3)
            max_rows(0, 0)
            pe.wait_ge(mrow_kept, 1)
            max_rows(0, 1)
            slot(0, 0, 0, 0)
            with pe.Fori(0, B - 1) as b:
                for i in range(1, LOOP + 1):
                    slot(b * PAIRS + i, i % PAIRS, b * 2 + i // 2, b)
            for n in range(NS - 3, NS):
                slot(n, n % PAIRS, n // 2, B - 1)
            weigh(NS - 1, T - 1, 1, NS // 2)
            sums(NS - 1)
            pe.wait_ge(o_normed, NS)
            for i in range(T):
                project_out(B - 1, i)


def graph_attention_kernel(nc, x, adj, Wq, bq, Wk, bk, Wv, bv, Wo, bo, out):
    sh = Shapes(x, heads=8)
    with ExitStack() as ctx:
        def sb(name, shape, dt):
            return ctx.enter_context(nc.sbuf_tensor(name, shape, dt))

        keep = (
            sb("mask", [P, sh.T, sh.N], F32),
            sb("maskT", [P, sh.T, sh.N], BF16),
            sb("Wo_hi", [P, sh.C, sh.D], F32R),
            sb("Wo_lo", [P, sh.C, sh.D], F32R),
            sb("bo_bc", [P, sh.D], F32),
            sb("ident", [P, P], F32),
            sb("identb", [P, P], BF16),
        )
        qk_d = nc.dram_tensor("qk_scratch", [sh.B, sh.PAIRS, 4, P, sh.N], F32).ap()
        v_d = nc.dram_tensor("v_scratch", [sh.B, sh.PAIRS, P, sh.T * P], F32).ap()
        io = (x, adj, Wq, bq, Wk, bk, Wv, bv, Wo, bo)
        project_stage(nc, sh, ctx, io, (qk_d, v_d), keep)
        attend_stage(nc, sh, io, (qk_d, v_d), keep, out)


_INS = ["x", "adj"] + [f"L0_gnn_{n}" for n in ("Wq", "bq", "Wk", "bk", "Wv", "bv", "Wo", "bo")]


def kernel(**inputs):
    import numpy as _np
    import concourse.bacc as _bacc
    from concourse import mybir as _mybir
    from concourse.bass_utils import run_bass_kernel_spmd as _run

    nc = _bacc.Bacc("TRN2", target_bir_lowering=False, num_devices=1)
    arrays, args = {}, []
    for name in _INS:
        a = _np.ascontiguousarray(inputs[name])
        arrays[f"in_{name}"] = a
        args.append(nc.dram_tensor(f"in_{name}", a.shape, _mybir.dt.from_np(a.dtype), kind="ExternalInput").ap())
    out = nc.dram_tensor("out_0", arrays["in_x"].shape, _mybir.dt.float32, kind="ExternalOutput").ap()
    graph_attention_kernel(nc, *args, out)
    r = _run(nc, [arrays], core_ids=[0])
    return r.results[0]["out_0"]
```

```python
from contextlib import ExitStack

import concourse.bass as bass
from concourse import mybir

ALU = mybir.AluOpType
ACT = mybir.ActivationFunctionType
F32 = mybir.dt.float32
F32R = mybir.dt.float32r
BF16 = mybir.dt.bfloat16

P = 128
EPS = 1e-5
NEG = 1e9
BIG = 2.0 ** 30
BANK = 512
MX_OF_STEP = [0, 0, 3, 3, 3, 3, 4, 0]
MROW_A_STEP, MROW_B_STEP = 5, 7
TILES_OF_STEP = [[], [], [], [0, 1], [2, 3], [4], [5, 6], [7]]
TILES_AFTER_MROW_A = [4, 5, 6, 7]


class Shapes:
    def __init__(self, x, heads):
        self.B, self.N, self.D = x.shape
        self.H = heads
        self.HD = self.D // heads
        self.C = self.D // P
        self.T = self.N // P
        self.PAIRS = heads // 2
        self.HALVES = self.N // BANK
        assert self.HD == 64 and self.N == 1024 and self.D == BANK and self.PAIRS == self.C


def after(eng, sem, count):
    if isinstance(count, int) and count <= 0:
        return
    eng.wait_ge(sem, count)


def wait_apart(eng, sem, count, passed):
    eng.wait_ge(sem, count)
    eng.sem_inc(passed, 1)


def halves(n=2):
    return [(h, slice(h * BANK, (h + 1) * BANK)) for h in range(n)]


def project_stage(nc, sh, ctx_outer, io, scratch, keep):
    x, adj, Wq, bq, Wk, bk, Wv, bv, Wo, bo = io
    qk_d, v_d = scratch
    mask, maskT, Wo_hi, Wo_lo, bo_bc, ident, identb = keep
    B, C, T, PAIRS = sh.B, sh.C, sh.T, sh.PAIRS
    J = 2 * PAIRS
    with ExitStack() as ctx:
        def sb(name, shape, dt):
            return ctx.enter_context(nc.sbuf_tensor(name, shape, dt))

        def sem(name):
            return ctx.enter_context(nc.semaphore(name))

        W_hi = [sb(f"w{n}_hi", [P, C, sh.D], F32R) for n in "qkv"] + [Wo_hi]
        W_lo = [sb(f"w{n}_lo", [P, C, sh.D], F32R) for n in "qkv"] + [Wo_lo]
        xs = sb("xs", [P, T, sh.D], F32)
        adj_sb = sb("adj_sb", [P, 2, sh.N], F32)
        hT_hi = sb("hT_hi", [P, C, sh.N], F32R)
        hT_lo = sb("hT_lo", [P, C, sh.N], F32R)
        hi_out = sb("hi_out", [P, 2, sh.N], F32R)
        lo_out = sb("lo_out", [P, 2, sh.N], F32R)
        v_out = sb("v_out", [P, PAIRS, T, P], F32)
        bv_bc = sb("bv_bc", [P, sh.D], F32)
        bqk = sb("bqk", [P, PAIRS, 2], F32)
        stats = sb("stats", [P, T, 6], F32)
        mv = sb("mv", [P, T, 2], F32)
        ve = sb("ve", [P, T], F32)
        rv = sb("rv", [P, T], F32)
        y0 = sb("y0", [P, T], F32)
        t1 = sb("t1", [P, T], F32)
        t2 = sb("t2", [P, T], F32)
        t3 = sb("t3", [P, T], F32)
        rstd = sb("rstd", [P, T], F32)
        nmr = sb("nmr", [P, T], F32)
        tp = ctx.enter_context(nc.psum_tensor("tp", [P, 2, BANK], F32))
        qk_ps = ctx.enter_context(nc.psum_tensor("qk_ps", [P, 2, sh.N], F32))
        v_ps = ctx.enter_context(nc.psum_tensor("v_ps", [P, 2, BANK], F32))

        w_loaded = [sem(f"w_loaded{i}") for i in range(4)]
        bias_loaded = sem("bias_loaded")
        adj_loaded = [sem(f"adj_loaded{i}") for i in range(2)]
        x_loaded = sem("x_loaded")
        zeroed = sem("zeroed")
        ident_made = sem("ident_made")
        identb_made = sem("identb_made")
        bias_scaled = sem("bias_scaled")
        w_hi_made = sem("w_hi_made")
        w_lo_made = sem("w_lo_made")
        adj_turned = sem("adj_turned")
        maskT_made = sem("maskT_made")
        mask_made = sem("mask_made")
        ln_steps = sem("ln_steps")
        sqrt_made = sem("sqrt_made")
        stats_passed = sem("stats_passed")
        h_made = sem("h_made")
        h_turned = sem("h_turned")
        hT_hi_made = sem("hT_hi_made")
        hT_lo_made = sem("hT_lo_made")
        qk_ready = sem("qk_ready")
        qk_hi_made = sem("qk_hi_made")
        qk_lo_made = sem("qk_lo_made")
        v_ready = sem("v_ready")
        v_made = sem("v_made")
        qk_stored = [sem(f"qk_stored{i}") for i in range(2)]
        v_stored = sem("v_stored")

        v_flat = v_out[:, :, :, :].rearrange("p a t n -> p (a t n)").rearrange("p (w c n) -> p w c n", w=2, c=C)
        W_raw = [xs[:, 0:C, :], xs[:, C:2 * C, :], v_flat[:, 0], v_flat[:, 1]]
        W_scale = [1.0 / 8.0, 1.0, 1.0, 1.0]
        LN_OPS = 2 * T + 7

        block = ctx.enter_context(nc.Block())

        @block.sync
        def _(sp):
            for i, w in enumerate((Wq, Wk, Wv, Wo)):
                sp.dma_start(W_raw[i], w.rearrange("(c p) n -> p c n", p=P)).then_inc(w_loaded[i], 16)
            with nc.allow_non_contiguous_dma(reason="two vectors of 512, once"):
                sp.dma_start(bqk[:, :, 0], bq.rearrange("(c p) -> p c", p=P)).then_inc(bias_loaded, 16)
                sp.dma_start(bqk[:, :, 1], bk.rearrange("(c p) -> p c", p=P)).then_inc(bias_loaded, 16)
            sp.dma_start(bv_bc[:, :], bv.rearrange("(a n) -> a n", a=1).partition_broadcast(P)).then_inc(bias_loaded, 16)
            sp.dma_start(bo_bc[:, :], bo.rearrange("(a n) -> a n", a=1).partition_broadcast(P)).then_inc(bias_loaded, 16)
            for t in range(T):
                if t == 2:
                    sp.wait_ge(w_lo_made, 2)
                    sp.dma_start(xs[:, :, :], x[0].rearrange("(t p) n -> p t n", p=P)).then_inc(x_loaded, 16)
                after(sp, maskT_made, 2 * (t - 1))
                after(sp, mask_made, t - 1)
                sp.dma_start(adj_sb[:, t % 2, :], adj[t * P:(t + 1) * P, :]).then_inc(adj_loaded[t % 2], 16)

            def step(b, last):
                if not last:
                    sp.wait_ge(h_turned, b * T + T)
                    sp.dma_start(xs[:, :, :], x[b + 1].rearrange("(t p) n -> p t n", p=P)).then_inc(x_loaded, 16)
                for j in range(J):
                    sp.wait_ge(qk_hi_made, b * J + (j + 1))
                    sp.dma_start(qk_d[b, j // 2, 2 * (j % 2)], hi_out[:, j % 2, :].bitcast(F32)).then_inc(qk_stored[j % 2], 16)
                    sp.wait_ge(qk_lo_made, b * J + (j + 1))
                    sp.dma_start(qk_d[b, j // 2, 2 * (j % 2) + 1], lo_out[:, j % 2, :].bitcast(F32)).then_inc(qk_stored[j % 2], 16)
                sp.wait_ge(v_made, b * T + T)
                sp.dma_start(v_d[b].rearrange("a p n -> p a n"),
                             v_out[:, :, :, :].rearrange("p a t n -> p a (t n)")).then_inc(v_stored, 16)

            with sp.Fori(0, B - 1) as b:
                step(b, False)
            step(B - 1, True)
            for i in range(2):
                sp.wait_ge(qk_stored[i], 32 * (J // 2) * B)
            sp.wait_ge(v_stored, 16 * B)

        @block.gpsimd
        def _(pool):
            nc.gpsimd.memset(ident[:, :], 0.0).then_inc(zeroed, 1)
            pool.wait_ge(zeroed, 1)
            nc.gpsimd.affine_select(out=ident[:, :], in_=ident[:, :], compare_op=ALU.not_equal, fill=1.0, base=0,
                                    pattern=[[-1, P]], channel_multiplier=1).then_inc(ident_made, 1)

        @block.scalar
        def _(act):
            for i in range(4):
                act.wait_ge(w_loaded[i], 16)
                nc.scalar.mul(W_hi[i][:, :, :], W_raw[i], W_scale[i]).then_inc(w_hi_made, 1)

            def relu_ln(b):
                act.wait_ge(ln_steps, b * LN_OPS + 2 * T + 2)
                nc.scalar.activation(y0[:, :], rv[:, :], ACT.Sqrt).then_inc(sqrt_made, 1)
                act.wait_ge(ln_steps, b * LN_OPS + LN_OPS)
                for t in range(T):
                    nc.scalar.activation(xs[:, t, :], xs[:, t, :], ACT.Relu, bias=nmr[:, t:t + 1],
                                         scale=rstd[:, t:t + 1]).then_inc(h_made, 1)

            def step(b, last):
                for t in range(T):
                    act.wait_ge(h_turned, b * T + (t + 1))
                    nc.scalar.copy(hT_hi[:, :, t * P:(t + 1) * P],
                                   tp[:, t % 2, :].rearrange("p (c n) -> p c n", c=C)).then_inc(hT_hi_made, 1)
                for j in range(J):
                    act.wait_ge(qk_ready, b * J + (j + 1))
                    after(act, qk_stored[j % 2], b * (32 * (J // 2)) + 32 * (j // 2))
                    nc.scalar.activation(hi_out[:, j % 2, :], qk_ps[:, j % 2, :], ACT.Identity,
                                         bias=bqk[:, j // 2, j % 2:j % 2 + 1]).then_inc(qk_hi_made, 1)
                    if j == 3 and not last:
                        relu_ln(b + 1)

            act.wait_ge(bias_scaled, 1)
            relu_ln(0)
            first_then_loop(act, B, step)

        @block.vector
        def _(dve):
            for i in range(4):
                dve.wait_ge(w_hi_made, i + 1)
                nc.vector.scalar_tensor_tensor(out=W_lo[i][:, :, :].rearrange("p c n -> p (c n)"),
                                               in0=W_raw[i].rearrange("p c n -> p (c n)"), scalar=W_scale[i],
                                               in1=W_hi[i][:, :, :].bitcast(F32).rearrange("p c n -> p (c n)"),
                                               op0=ALU.mult, op1=ALU.subtract).then_inc(w_lo_made, 1)
            dve.wait_ge(bias_loaded, 64)
            nc.vector.tensor_scalar(bqk[:, :, 0], bqk[:, :, 0], W_scale[0], None, ALU.mult).then_inc(bias_scaled, 1)
            dve.wait_ge(ident_made, 1)
            nc.vector.tensor_copy(identb[:, :], ident[:, :]).then_inc(identb_made, 1)

            def layer_norm(b):
                at = b * LN_OPS
                dve.wait_ge(x_loaded, b * 16 + 16)
                for t in range(T):
                    nc.vector.bn_stats(stats[:, t, :], xs[:, t, :]).then_inc(ln_steps, 1)
                wait_apart(dve, ln_steps, at + T, stats_passed)
                for t in range(T):
                    nc.vector.bn_aggr(mv[:, t, :], stats[:, t, :]).then_inc(ln_steps, 1)
                dve.wait_ge(ln_steps, at + 2 * T)
                nc.vector.tensor_scalar(ve[:, :], mv[:, :, 1], EPS, None, ALU.add).then_inc(ln_steps, 1)
                dve.wait_ge(ln_steps, at + 2 * T + 1)
                nc.vector.reciprocal(rv[:, :], ve[:, :]).then_inc(ln_steps, 1)
                dve.wait_ge(sqrt_made, b + 1)
                nc.vector.tensor_tensor(t1[:, :], y0[:, :], y0[:, :], ALU.mult).then_inc(ln_steps, 1)
                dve.wait_ge(ln_steps, at + 2 * T + 3)
                nc.vector.tensor_tensor(t2[:, :], t1[:, :], ve[:, :], ALU.mult).then_inc(ln_steps, 1)
                dve.wait_ge(ln_steps, at + 2 * T + 4)
                nc.vector.tensor_scalar(t3[:, :], t2[:, :], -0.5, 1.5, ALU.mult, ALU.add).then_inc(ln_steps, 1)
                dve.wait_ge(ln_steps, at + 2 * T + 5)
                nc.vector.tensor_tensor(rstd[:, :], y0[:, :], t3[:, :], ALU.mult).then_inc(ln_steps, 1)
                dve.wait_ge(ln_steps, at + 2 * T + 6)
                nc.vector.scalar_tensor_tensor(out=nmr[:, :], in0=mv[:, :, 0], scalar=-1.0, in1=rstd[:, :],
                                               op0=ALU.mult, op1=ALU.mult).then_inc(ln_steps, 1)

            for t in range(T):
                for h in range(2):
                    dve.wait_ge(adj_turned, 2 * t + h + 1)
                    nc.vector.tensor_scalar(maskT[:, 4 * h:4 * h + 4, t * P:(t + 1) * P],
                                            v_ps[:, h, :].rearrange("p (k n) -> p k n", k=4), -1.0, None,
                                            ALU.add).then_inc(maskT_made, 1)
                nc.vector.tensor_scalar(mask[:, t, :], adj_sb[:, t % 2, :], -1.0, BIG, ALU.add,
                                        ALU.mult).then_inc(mask_made, 1)
                if t == 1:
                    layer_norm(0)

            def step(b, last):
                for t in range(T):
                    dve.wait_ge(hT_hi_made, b * T + (t + 1))
                    cols = slice(t * P, (t + 1) * P)
                    nc.vector.tensor_tensor(hT_lo[:, :, cols], tp[:, t % 2, :].rearrange("p (c n) -> p c n", c=C),
                                            hT_hi[:, :, cols].bitcast(F32), ALU.subtract).then_inc(hT_lo_made, 1)
                for j in range(J):
                    dve.wait_ge(qk_hi_made, b * J + (j + 1))
                    nc.vector.scalar_tensor_tensor(out=lo_out[:, j % 2, :], in0=qk_ps[:, j % 2, :],
                                                   scalar=bqk[:, j // 2, j % 2:j % 2 + 1],
                                                   in1=hi_out[:, j % 2, :].bitcast(F32), op0=ALU.add,
                                                   op1=ALU.subtract).then_inc(qk_lo_made, 1)
                    if j == 2 and not last:
                        layer_norm(b + 1)
                after(dve, v_stored, b * 16)
                for t in range(T):
                    dve.wait_ge(v_ready, b * T + (t + 1))
                    nc.vector.tensor_tensor(v_out[:, :, t, :], v_ps[:, t % 2, :].rearrange("p (a n) -> p a n", a=PAIRS),
                                            bv_bc[:, :].rearrange("p (a n) -> p a n", a=PAIRS),
                                            ALU.add).then_inc(v_made, 1)

            first_then_loop(dve, B, step)

        @block.tensor
        def _(pe):
            pe.wait_ge(ident_made, 1)
            for t in range(T):
                pe.wait_ge(adj_loaded[t % 2], 16 * (t // 2 + 1))
                for h in range(2):
                    after(pe, maskT_made, 2 * (t - 1) + h + 1)
                    for i in range(4):
                        kt = 4 * h + i
                        mm = pe.transpose(v_ps[:, h, i * P:(i + 1) * P], adj_sb[:, t % 2, kt * P:(kt + 1) * P], ident[:, :])
                    mm.then_inc(adj_turned, 1)
            pe.wait_ge(w_lo_made, 4)
            pe.wait_ge(maskT_made, 2 * T)

            def three_passes(out, lhs, rhs, n):
                for c in range(n):
                    for k, (l, r) in enumerate(((0, 0), (0, 1), (1, 0))):
                        mm = pe.matmul(out, lhs(l, c), rhs(r, c), start=(c == 0 and k == 0), stop=(c == n - 1 and k == 2))
                return mm

            hT = (hT_hi, hT_lo)

            def step(b, last):
                for t in range(T):
                    pe.wait_ge(h_made, b * T + (t + 1))
                    after(pe, hT_lo_made, b * T + (t - 1))
                    for c in range(C):
                        mm = pe.transpose(tp[:, t % 2, c * P:(c + 1) * P], xs[:, t, c * P:(c + 1) * P], ident[:, :])
                    mm.then_inc(h_turned, 1)
                for j in range(J):
                    w = (W_hi[j % 2], W_lo[j % 2])
                    after(pe, qk_lo_made, b * J + (j - 1))
                    for h, cols in halves():
                        if j == 0:
                            pe.wait_ge(hT_lo_made, b * T + 4 * (h + 1))
                        mm = three_passes(qk_ps[:, j % 2, cols],
                                          lambda l, c: w[l][:, c, (j // 2) * P:(j // 2 + 1) * P],
                                          lambda r, c: hT[r][:, c, cols], C)
                    mm.then_inc(qk_ready, 1)
                for t in range(T):
                    after(pe, v_made, b * T + (t - 1))
                    mm = three_passes(v_ps[:, t % 2, :], lambda l, c: hT[l][:, c, t * P:(t + 1) * P],
                                      lambda r, c: (W_hi[2], W_lo[2])[r][:, c, :], C)
                    mm.then_inc(v_ready, 1)

            first_then_loop(pe, B, step)


def first_then_loop(eng, count, step):
    step(0, False)
    with eng.Fori(1, count - 1) as b:
        step(b, False)
    step(count - 1, True)


def weave(base, more):
    out, done = [], 0
    for i, item in enumerate(base):
        out.append(item)
        upto = len(more) * (i + 1) // len(base)
        out += more[done:upto]
        done = upto
    return out


def slot_order(T, behind, ahead, outs):
    items = []
    j = 0
    for s in range(T):
        pairs = [[("st", s, hd), ("exp", s, hd)] + ([("acc", s, hd)] if s else []) for hd in range(2)]
        w = [("w", s, h) for h in range(2)] if s or behind else []
        mx = []
        for _ in range(MX_OF_STEP[s] if ahead else 0):
            mx.append([("mx", j)] + ([("split", j // T)] if j % T == T - 1 else []))
            j += 1
        base = pairs[0] + sum(mx[:1], []) + pairs[1] + w[:1] + sum(mx[1:2], []) + w[1:] + sum(mx[2:], [])
        if behind and s == 0:
            base += [("copy_o",)]
        if behind and s == 1:
            base += [("sum",), ("recip",)]
        if behind and s == 2:
            base += [("norm",), ("high",)]
        if behind and s == 3:
            base = [("low",)] + base
        if ahead and s == MROW_A_STEP:
            items += pairs[0] + [("mrow", 0), ("keep", 0)]
            base = base[len(pairs[0]):]
        more = [("out", i, c) for i in (TILES_OF_STEP[s] if outs else []) for c in range(4)]
        if more:
            base = weave(base, more)
            for i in TILES_OF_STEP[s]:
                base.insert(base.index(("out", i, 0)), ("bo", i))
                base.insert(base.index(("out", i, 3)) + 1, ("add", i))
        if ahead and s == MROW_B_STEP:
            base += [("mrow", 1), ("keep", 1)]
        items += base
    return items


def attend_stage(nc, sh, io, scratch, keep, out):
    x = io[0]
    qk_d, v_d = scratch
    mask, maskT, Wo_hi, Wo_lo, bo_bc, ident, identb = keep
    B, N, D, T, PAIRS, HD = sh.B, sh.N, sh.D, sh.T, sh.PAIRS, sh.HD
    HT = 2 * T
    MROWS = 3
    KB_ROWS = HD + MROWS
    ADDS = 2 * (T - 1)
    RING = 4
    NS = B * PAIRS
    with ExitStack() as ctx:
        def sb(name, shape, dt):
            return ctx.enter_context(nc.sbuf_tensor(name, shape, dt))

        def sem(name):
            return ctx.enter_context(nc.semaphore(name))

        k_hl = sb("k_hl", [P, 2, 2, N], F32R)
        q_hh = sb("q_hh", [P, 2, 2, N], F32R)
        k_h1 = sb("k_h1", [P, 2, 2, N], F32R)
        q_lm = sb("q_lm", [P, 2, 2, N], F32R)
        v_sb = sb("v_sb", [P, 2, T, P], F32)
        probs = sb("probs", [P, 2, 2, N], F32)
        acc = sb("acc", [P, 2, N], F32)
        o_sb = sb("o_sb", [P, N], F32)
        rsum = sb("rsum", [P, N], F32)
        oT_hi = sb("oT_hi", [P, PAIRS, N], F32R)
        oT_lo = sb("oT_lo", [P, PAIRS, N], F32R)
        xy = sb("xy", [P, RING, D], F32)
        ones = sb("ones", [P, HD], F32)
        qmax = sb("qmax", [P, 2, T], F32)
        empty = sb("empty", [P, 2, T], F32)
        rest = sb("rest", [P, 2, T], F32)
        pieces = sb("pieces", [P, 2, T, KB_ROWS + 1], BF16)

        def pb(name, cols):
            return ctx.enter_context(nc.psum_tensor(name, [P, cols], F32))

        sc_ps = [pb(f"sc_ps{i}", N) for i in range(2)]
        o_ps = pb("o_ps", N)
        misc = pb("misc", N)

        qk_loaded = [sem(f"qk_loaded{i}") for i in range(2)]
        qk2_loaded = [sem(f"qk2_loaded{i}") for i in range(2)]
        v_loaded = [sem(f"v_loaded{i}") for i in range(2)]
        x_loaded = [sem(f"x2_loaded{i}") for i in range(RING)]
        y_stored = [sem(f"y_stored{i}") for i in range(RING)]
        consts = sem("consts")
        q_lm_zeroed = sem("q_lm_zeroed")
        sc_ready = sem("sc_ready")
        sc_read = sem("sc_read")
        mx_passed = sem("mx_passed")
        stores_passed = sem("stores_passed")
        m_steps = sem("m_steps")
        mrow_ready = sem("mrow_ready")
        mrow_kept = sem("mrow_kept")
        exp_done = sem("exp_done")
        pv_done = sem("pv_done")
        o_copied = sem("o_copied")
        added = sem("added")
        sum_ready = sem("sum_ready")
        log_taken = sem("log_taken")
        recip_ready = sem("recip_ready")
        o_normed = sem("o_normed")
        oT_hi_made = sem("oT_hi_made")
        oT_lo_made = sem("oT_lo_made")
        y_ready = sem("y_ready")
        xbo_made = sem("xbo_made")
        y_made = sem("y_made")

        block = ctx.enter_context(nc.Block())

        orders = {
            "first": slot_order(T, False, True, False),
            "outs": slot_order(T, True, True, True),
            "plain": slot_order(T, True, True, False),
            "last": slot_order(T, True, False, False),
        }

        def kind_of(n, p):
            if isinstance(n, int) and n in (0, NS - 1):
                return "first" if n == 0 else "last"
            return "outs" if p == 0 else "plain"

        def items_of(n, p):
            k = 0
            for item in orders[kind_of(n, p)]:
                yield item, k
                k += item[0] in ("st", "mx")

        def unit_of(n, p, item):
            return next(k for i, k in items_of(n, p) if i == item)

        UNITS = 2 * HT
        LEAD = HT

        def every_slot(eng, slot):
            slot(0, 0, 0, 0)
            with eng.Fori(0, B - 1) as b:
                for i in range(1, PAIRS + 1):
                    slot(b * PAIRS + i, i % PAIRS, b * 2 + i // 2, b)
            for n in range(NS - 3, NS):
                slot(n, n % PAIRS, n // 2, B - 1)

        @block.sync
        def _(sp):
            def load(b, pair, par, n):
                src = lambda i: qk_d[b, pair, i].rearrange("(h p) n -> p h n", h=2)
                lo, hi = slice(0, HD), slice(HD, P)
                QHI, QLO, KHI, KLO = range(4)
                for dst, rows, s in ((q_hh, lo, QHI), (k_hl, lo, KHI), (q_hh, hi, QHI), (k_hl, hi, KLO)):
                    sp.dma_start(dst[rows, par].bitcast(F32), src(s)).then_inc(qk_loaded[par], 16)
                for dst, s in ((k_h1, KHI), (q_lm, QLO)):
                    sp.dma_start(dst[lo, par].bitcast(F32), src(s)).then_inc(qk2_loaded[par], 16)
                after(sp, pv_done, n * T - T)
                sp.dma_start(v_sb[:, par].rearrange("p t n -> p (t n)"), v_d[b, pair]).then_inc(v_loaded[par], 16)

            def load_x(b, i):
                sp.dma_start(xy[:, i % RING, :], x[b, i * P:(i + 1) * P, :]).then_inc(x_loaded[i % RING], 16)

            def outs(b):
                for i in range(RING):
                    load_x(b, i)
                for i in range(T):
                    sp.wait_ge(y_made, b * T + (i + 1))
                    sp.dma_start(out[b, i * P:(i + 1) * P, :], xy[:, i % RING, :]).then_inc(y_stored[i % RING], 16)
                    if i >= 1 and i - 1 + RING < T:
                        sp.wait_ge(y_stored[(i - 1) % RING], b * (16 * T // RING) + 16 * ((i - 1) // RING + 1))
                        load_x(b, i - 1 + RING)
                for i in range(RING):
                    wait_apart(sp, y_stored[i], (b + 1) * (16 * T // RING), stores_passed)

            load(0, 0, 0, 0)

            def slot(n, p, half, b):
                kind = kind_of(n, p)
                if kind != "last":
                    if kind != "first":
                        sp.wait_ge(sc_ready, n * UNITS + LEAD)
                    load(next_batch(n, p, b), (p + 1) % PAIRS, (p + 1) % 2, n + 1)
                if kind == "outs":
                    outs(b)

            def next_batch(n, p, b):
                if isinstance(n, int):
                    return (n + 1) // PAIRS
                return b + 1 if p in (0, PAIRS - 1) else b

            every_slot(sp, slot)
            outs(B - 1)

        @block.gpsimd
        def _(pool):
            nc.gpsimd.memset(pieces[:, :, :, :], 0.0).then_inc(consts, 1)
            nc.gpsimd.memset(ones[:, :], 1.0).then_inc(consts, 1)
            pool.wait_ge(consts, 2)
            nc.gpsimd.memset(k_h1[HD:P, :, :, :].bitcast(F32), 1.0).then_inc(consts, 1)
            nc.gpsimd.memset(q_lm[HD:P, :, :, :].bitcast(F32), 0.0).then_inc(q_lm_zeroed, 1)
            pool.wait_ge(q_lm_zeroed, 1)

            def low_part(n, pair):
                pool.wait_ge(oT_hi_made, n + 1)
                nc.gpsimd.tensor_tensor(oT_lo[:, pair, :], o_sb[:, :], oT_hi[:, pair, :].bitcast(F32),
                                        ALU.subtract).then_inc(oT_lo_made, 1)

            def add_bo(b, i):
                pool.wait_ge(x_loaded[i % RING], b * (16 * T // RING) + 16 * (i // RING + 1))
                nc.gpsimd.tensor_tensor(xy[:, i % RING, :], xy[:, i % RING, :], bo_bc[:, :],
                                        ALU.add).then_inc(xbo_made, 1)

            def slot(n, p, half, b):
                for item, _ in items_of(n, p):
                    if item[0] == "acc":
                        _, t, hd = item
                        pool.wait_ge(exp_done, n * HT + (2 * t + hd + 1))
                        if t == 1:
                            after(pool, sum_ready, n)
                            first = probs[:, 0, hd, :]
                        else:
                            pool.wait_ge(added, n * ADDS + (2 * (t - 2) + hd + 1))
                            first = acc[:, hd, :]
                        nc.gpsimd.tensor_tensor(acc[:, hd, :], first, probs[:, t % 2, hd, :], ALU.add).then_inc(added, 1)
                    if item[0] == "low":
                        low_part(n - 1, (p - 1) % PAIRS)
                    if item[0] == "bo":
                        add_bo(b, item[1])

            every_slot(pool, slot)
            low_part(NS - 1, PAIRS - 1)
            for i in range(T):
                add_bo(B - 1, i)

        @block.scalar
        def _(act):
            nc.scalar.preload_act_table_set("natural_log_exp_and_others")

            def keep_mrows(n, par, hd):
                act.wait_ge(mrow_ready, n * 2 + (hd + 1))
                nc.scalar.copy(q_lm[HD:KB_ROWS, par, hd, :], misc[HD:KB_ROWS, :]).then_inc(mrow_kept, 1)

            def copy_o(n):
                act.wait_ge(pv_done, n * T + T)
                nc.scalar.copy(o_sb[:, :], o_ps[:, :]).then_inc(o_copied, 1)

            def recip(n):
                act.wait_ge(sum_ready, n + 1)
                nc.scalar.activation(rsum[:, :], misc[:, :], ACT.Ln).then_inc(log_taken, 1)
                act.wait_ge(log_taken, n + 1)
                nc.scalar.activation(rsum[:, :], rsum[:, :], ACT.Exp, scale=-1.0).then_inc(recip_ready, 1)

            def high_part(n, pair):
                act.wait_ge(o_normed, n + 1)
                nc.scalar.copy(oT_hi[:, pair, :], o_sb[:, :]).then_inc(oT_hi_made, 1)

            def slot(n, p, half, b):
                for item, k in items_of(n, p):
                    if item[0] == "exp":
                        _, s, hd = item
                        act.wait_ge(sc_read, n * UNITS + (LEAD + unit_of(n, p, ("st", s, hd)) + 1))
                        pr = probs[:, s % 2, hd, :]
                        nc.scalar.activation(pr, pr, ACT.Exp).then_inc(exp_done, 1)
                    if item[0] == "copy_o":
                        copy_o(n - 1)
                    if item[0] == "recip":
                        recip(n - 1)
                    if item[0] == "high":
                        high_part(n - 1, (p - 1) % PAIRS)
                    if item[0] == "keep":
                        keep_mrows(n + 1, (p + 1) % 2, item[1])

            act.wait_ge(q_lm_zeroed, 1)
            keep_mrows(0, 0, 0)
            keep_mrows(0, 0, 1)
            every_slot(act, slot)
            copy_o(NS - 1)
            recip(NS - 1)
            high_part(NS - 1, PAIRS - 1)

        @block.vector
        def _(dve):
            def mask_scores(n, s, hd, k):
                dve.wait_ge(sc_ready, n * UNITS + (LEAD + k + 1))
                after(dve, pv_done, n * T + (s - 1))
                t = max(s - 2, 1) if s >= 2 else T + s - 2
                after(dve, added, n * ADDS + (2 * (t - 1) + hd + 1 - (ADDS if s < 2 else 0)))
                nc.vector.scalar_tensor_tensor(out=probs[:, s % 2, hd, :], in0=maskT[:, s, :], scalar=NEG,
                                               in1=sc_ps[k % 2][:, :], op0=ALU.mult, op1=ALU.add).then_inc(sc_read, 1)

            def take_max(at, j, place):
                wait_apart(dve, sc_ready, at + 1, mx_passed)
                ps = sc_ps[place][:, :]
                nc.vector.tensor_tensor_reduce(ps, ps, mask[:, j % T, :], 1.0, -3.0e38, ALU.add, ALU.max,
                                               qmax[:, j // T, j % T:j % T + 1]).then_inc(sc_read, 1)

            def split_max(n, hd, at):
                piece = [pieces[:, hd, :, HD + i] for i in range(MROWS)]
                q, e = qmax[:, hd, :], empty[:, hd, :]
                done = n * 12 + 6 * hd
                dve.wait_ge(sc_read, at)
                nc.vector.tensor_scalar(e, q, -BIG / 2, BIG - NEG, ALU.is_lt, ALU.mult).then_inc(m_steps, 1)
                dve.wait_ge(m_steps, done + 1)
                nc.vector.tensor_tensor(q, q, e, ALU.add).then_inc(m_steps, 1)
                dve.wait_ge(m_steps, done + 2)
                after(dve, mrow_ready, n * 2 + (hd - 1))
                nc.vector.tensor_scalar(piece[0], q, -1.0, None, ALU.mult).then_inc(m_steps, 1)
                dve.wait_ge(m_steps, done + 3)
                nc.vector.scalar_tensor_tensor(out=rest[:, hd, :], in0=q, scalar=-1.0, in1=piece[0],
                                               op0=ALU.mult, op1=ALU.subtract).then_inc(m_steps, 1)
                dve.wait_ge(m_steps, done + 4)
                nc.vector.tensor_copy(piece[1], rest[:, hd, :]).then_inc(m_steps, 1)
                dve.wait_ge(m_steps, done + 5)
                nc.vector.tensor_tensor(piece[2], rest[:, hd, :], piece[1], ALU.subtract).then_inc(m_steps, 1)

            def norm(n):
                dve.wait_ge(recip_ready, n + 1)
                nc.vector.tensor_tensor(o_sb[:, :], o_sb[:, :], rsum[:, :], ALU.mult).then_inc(o_normed, 1)

            def add_out(b, i):
                dve.wait_ge(y_ready, b * T + (i + 1))
                dve.wait_ge(xbo_made, b * T + (i + 1))
                nc.vector.tensor_tensor(xy[:, i % RING, :], misc[:, (i % 2) * BANK:(i % 2 + 1) * BANK],
                                        xy[:, i % RING, :], ALU.add).then_inc(y_made, 1)

            def slot(n, p, half, b):
                for item, k in items_of(n, p):
                    if item[0] == "st":
                        mask_scores(n, item[1], item[2], k)
                    if item[0] == "mx":
                        take_max(n * UNITS + (LEAD + k), item[1], k % 2)
                    if item[0] == "split":
                        split_max(n + 1, item[1], n * UNITS + (LEAD + k))
                    if item[0] == "norm":
                        norm(n - 1)
                    if item[0] == "add":
                        add_out(b, item[1])

            dve.wait_ge(consts, 1)
            for j in range(HT):
                take_max(j, j, j % 2)
                if j % T == T - 1:
                    split_max(0, j // T, j + 1)
            every_slot(dve, slot)
            norm(NS - 1)
            for i in range(T):
                add_out(B - 1, i)

        @block.tensor
        def _(pe):
            def query_scores(at, j, place, par):
                hd, qt = j // T, j % T
                after(pe, sc_read, at - 1)
                for h, cols in halves():
                    mm = pe.matmul(sc_ps[place][:, cols], q_hh[:, par, hd, qt * P:(qt + 1) * P],
                                   k_hl[:, par, hd, cols], start=True, stop=True)
                mm.then_inc(sc_ready, 1)

            def max_rows(n, hd):
                pe.wait_ge(m_steps, n * 12 + 6 * (hd + 1))
                for qt in range(T):
                    mm = pe.matmul(misc[0:KB_ROWS, qt * P:(qt + 1) * P], pieces[:, hd, qt, 0:KB_ROWS], identb[:, :],
                                   start=True, stop=True)
                mm.then_inc(mrow_ready, 1)

            def key_scores(n, s, hd, par, loads, k):
                if s == 0:
                    pe.wait_ge(mrow_kept, n * 2 + (hd + 1))
                    if hd == 0:
                        pe.wait_ge(qk2_loaded[par], loads * 32)
                after(pe, sc_read, n * UNITS + (LEAD + k - 1))
                keys = slice(s * P, (s + 1) * P)
                ps = sc_ps[k % 2]
                for h, cols in halves():
                    pe.matmul(ps[:, cols], k_hl[:, par, hd, keys], q_hh[:, par, hd, cols], start=True, stop=False)
                for h, cols in halves():
                    mm = pe.matmul(ps[:, cols], k_h1[:, par, hd, keys], q_lm[:, par, hd, cols], start=False, stop=True)
                mm.then_inc(sc_ready, 1)

            def weigh(n, s, h, par, loads):
                if s == 0 and h == 0:
                    pe.wait_ge(v_loaded[par], loads * 16)
                    after(pe, o_copied, n)
                if h == 0:
                    pe.wait_ge(exp_done, n * HT + (2 * s + 2))
                cols = slice(h * BANK, (h + 1) * BANK)
                for hd in range(2):
                    rows = slice(hd * HD, (hd + 1) * HD)
                    mm = pe.matmul(o_ps[rows, cols], v_sb[:, par, s, rows], probs[:, s % 2, hd, cols],
                                   start=(s == 0), stop=(s == T - 1))
                if h == 1:
                    mm.then_inc(pv_done, 1)

            def sums(n):
                pe.wait_ge(added, n * ADDS + ADDS)
                for h, cols in halves():
                    for hd in range(2):
                        rows = slice(hd * HD, (hd + 1) * HD)
                        mm = pe.matmul(misc[rows, cols], ones[:, :], acc[:, hd, cols], start=True, stop=True)
                mm.then_inc(sum_ready, 1)

            def project_out(b, i, c):
                toks = slice(i * P, (i + 1) * P)
                o = misc[:, (i % 2) * BANK:(i % 2 + 1) * BANK]
                if i == 0 and c == 0:
                    pe.wait_ge(oT_lo_made, b * PAIRS + PAIRS)
                if i >= 2 and c == 0:
                    pe.wait_ge(y_made, b * T + (i - 1))
                for k, (l, r) in enumerate(((oT_hi, Wo_hi), (oT_hi, Wo_lo), (oT_lo, Wo_hi))):
                    mm = pe.matmul(o, l[:, c, toks], r[:, c, :], start=(c == 0 and k == 0),
                                   stop=(c == PAIRS - 1 and k == 2))
                if c == PAIRS - 1:
                    mm.then_inc(y_ready, 1)

            def slot(n, p, half, b):
                par, nxt = p % 2, (p + 1) % 2
                loads = half + 1
                loads_next = loads + par
                loads_prev = half + par
                tiles = 0
                for item, k in items_of(n, p):
                    if item[0] == "st":
                        key_scores(n, item[1], item[2], par, loads, k)
                    if item[0] == "mx":
                        if item[1] == 0:
                            pe.wait_ge(qk_loaded[nxt], loads_next * 64)
                        query_scores(n * UNITS + (LEAD + k), item[1], k % 2, nxt)
                    if item[0] == "w":
                        _, s, h = item
                        if s == 0:
                            weigh(n - 1, T - 1, h, nxt, loads_prev)
                        else:
                            weigh(n, s - 1, h, par, loads)
                    if item[0] == "sum":
                        sums(n - 1)
                    if item[0] == "mrow":
                        after(pe, log_taken, n)
                        if item[1] == 1:
                            pe.wait_ge(mrow_kept, n * 2 + 3)
                        if tiles:
                            pe.wait_ge(y_made, b * T + tiles)
                        max_rows(n + 1, item[1])
                    if item[0] == "out":
                        _, i, c = item
                        if c == 0:
                            pe.wait_ge(log_taken, n)
                            if i in TILES_AFTER_MROW_A:
                                pe.wait_ge(mrow_kept, n * 2 + 3)
                        project_out(b, i, c)
                        tiles = i + 1

            pe.wait_ge(qk_loaded[0], 64)
            for j in range(HT):
                query_scores(j, j, j % 2, 0)
            pe.wait_ge(consts, 3)
            max_rows(0, 0)
            pe.wait_ge(mrow_kept, 1)
            max_rows(0, 1)
            every_slot(pe, slot)
            for h in range(2):
                weigh(NS - 1, T - 1, h, 1, NS // 2)
            sums(NS - 1)
            pe.wait_ge(log_taken, NS)
            for i in range(T):
                for c in range(PAIRS):
                    project_out(B - 1, i, c)


def graph_attention_kernel(nc, x, adj, Wq, bq, Wk, bk, Wv, bv, Wo, bo, out):
    sh = Shapes(x, heads=8)
    with ExitStack() as ctx:
        def sb(name, shape, dt):
            return ctx.enter_context(nc.sbuf_tensor(name, shape, dt))

        keep = (
            sb("mask", [P, sh.T, sh.N], BF16),
            sb("maskT", [P, sh.T, sh.N], BF16),
            sb("Wo_hi", [P, sh.C, sh.D], F32R),
            sb("Wo_lo", [P, sh.C, sh.D], F32R),
            sb("bo_bc", [P, sh.D], F32),
            sb("ident", [P, P], F32),
            sb("identb", [P, P], BF16),
        )
        qk_d = nc.dram_tensor("qk_scratch", [sh.B, sh.PAIRS, 4, P, sh.N], F32).ap()
        v_d = nc.dram_tensor("v_scratch", [sh.B, sh.PAIRS, P, sh.T * P], F32).ap()
        io = (x, adj, Wq, bq, Wk, bk, Wv, bv, Wo, bo)
        project_stage(nc, sh, ctx, io, (qk_d, v_d), keep)
        attend_stage(nc, sh, io, (qk_d, v_d), keep, out)


_INS = ["x", "adj"] + [f"L0_gnn_{n}" for n in ("Wq", "bq", "Wk", "bk", "Wv", "bv", "Wo", "bo")]


def kernel(**inputs):
    import numpy as _np
    import concourse.bacc as _bacc
    from concourse import mybir as _mybir
    from concourse.bass_utils import run_bass_kernel_spmd as _run

    nc = _bacc.Bacc("TRN2", target_bir_lowering=False, num_devices=1)
    arrays, args = {}, []
    for name in _INS:
        a = _np.ascontiguousarray(inputs[name])
        arrays[f"in_{name}"] = a
        args.append(nc.dram_tensor(f"in_{name}", a.shape, _mybir.dt.from_np(a.dtype), kind="ExternalInput").ap())
    out = nc.dram_tensor("out_0", arrays["in_x"].shape, _mybir.dt.float32, kind="ExternalOutput").ap()
    graph_attention_kernel(nc, *args, out)
    r = _run(nc, [arrays], core_ids=[0])
    return r.results[0]["out_0"]
```

```python
from contextlib import ExitStack

import concourse.bass as bass
from concourse import mybir

ALU = mybir.AluOpType
ACT = mybir.ActivationFunctionType
F32 = mybir.dt.float32
F32R = mybir.dt.float32r
BF16 = mybir.dt.bfloat16

P = 128
EPS = 1e-5
NEG = 1e9
BIG = 119 * 2.0 ** 23
BANK = 512
STEPS = {
    "plain": ["ssww", "smsmwwmmzmm", "nwmswmsm", "ssmwmw", "swsw",
              "smmwmswm", "smwsw", "rssww"],
    "outs": ["ssww", "ssmwwmm", "wssmw", "sswwmmzm", "wsnosomomomow",
             "osooosoomwomooomwomo", "oswsomwmo", "ossooorww"],
    "after": ["sswmwm", "sswmoomwmomo", "swmws", "ososoomzmnwmmw", "sswmw",
              "msmswmwm", "swws", "rssww"],
}
PLACES = 3
SPLIT_STEPS = 6


class Shapes:
    def __init__(self, x, heads):
        self.B, self.N, self.D = x.shape
        self.H = heads
        self.HD = self.D // heads
        self.C = self.D // P
        self.T = self.N // P
        self.PAIRS = heads // 2
        self.HALVES = self.N // BANK
        assert self.T == 2 * self.PAIRS and self.HD == 64 and self.N == 1024 and self.D == BANK and self.PAIRS == self.C


def after(eng, sem, count):
    if isinstance(count, int) and count <= 0:
        return
    eng.wait_ge(sem, count)


def wait_apart(eng, sem, count, passed):
    eng.wait_ge(sem, count)
    eng.sem_inc(passed, 1)


def halves(n=2):
    return [(h, slice(h * BANK, (h + 1) * BANK)) for h in range(n)]


def project_stage(nc, sh, ctx_outer, io, scratch, keep):
    x, adj, Wq, bq, Wk, bk, Wv, bv, Wo, bo = io
    qk_d, v_d = scratch
    mask, maskT, Wo_hi, Wo_lo, bo_bc, ident, identb = keep
    B, C, T, PAIRS = sh.B, sh.C, sh.T, sh.PAIRS
    J = 2 * PAIRS
    with ExitStack() as ctx:
        def sb(name, shape, dt):
            return ctx.enter_context(nc.sbuf_tensor(name, shape, dt))

        def sem(name):
            return ctx.enter_context(nc.semaphore(name))

        W_hi = [sb(f"w{n}_hi", [P, C, sh.D], F32R) for n in "qkv"] + [Wo_hi]
        W_lo = [sb(f"w{n}_lo", [P, C, sh.D], F32R) for n in "qkv"] + [Wo_lo]
        xs = sb("xs", [P, T, sh.D], F32)
        adj_sb = sb("adj_sb", [P, 2, sh.N], F32)
        hT_hi = sb("hT_hi", [P, C, sh.N], F32R)
        hT_lo = sb("hT_lo", [P, C, sh.N], F32R)
        hi_out = sb("hi_out", [P, 2, sh.N], F32R)
        lo_out = sb("lo_out", [P, 2, sh.N], F32R)
        v_out = sb("v_out", [P, PAIRS, T, P], F32)
        bv_bc = sb("bv_bc", [P, sh.D], F32)
        bqk = sb("bqk", [P, PAIRS, 2], F32)
        stats = sb("stats", [P, T, 6], F32)
        mv = sb("mv", [P, T, 2], F32)
        ve = sb("ve", [P, T], F32)
        rv = sb("rv", [P, T], F32)
        y0 = sb("y0", [P, T], F32)
        t1 = sb("t1", [P, T], F32)
        t2 = sb("t2", [P, T], F32)
        t3 = sb("t3", [P, T], F32)
        rstd = sb("rstd", [P, T], F32)
        nmr = sb("nmr", [P, T], F32)
        tp = ctx.enter_context(nc.psum_tensor("tp", [P, 2, BANK], F32))
        qk_ps = ctx.enter_context(nc.psum_tensor("qk_ps", [P, 2, sh.N], F32))
        v_ps = ctx.enter_context(nc.psum_tensor("v_ps", [P, 2, BANK], F32))

        w_loaded = [sem(f"w_loaded{i}") for i in range(4)]
        bias_loaded = sem("bias_loaded")
        adj_loaded = [sem(f"adj_loaded{i}") for i in range(2)]
        x_loaded = sem("x_loaded")
        zeroed = sem("zeroed")
        ident_made = sem("ident_made")
        identb_made = sem("identb_made")
        bias_scaled = sem("bias_scaled")
        w_hi_made = sem("w_hi_made")
        w_lo_made = sem("w_lo_made")
        adj_turned = sem("adj_turned")
        maskT_made = sem("maskT_made")
        mask_made = sem("mask_made")
        ln_steps = sem("ln_steps")
        sqrt_made = sem("sqrt_made")
        stats_passed = sem("stats_passed")
        h_made = sem("h_made")
        h_turned = sem("h_turned")
        hT_hi_made = sem("hT_hi_made")
        hT_lo_made = sem("hT_lo_made")
        qk_ready = sem("qk_ready")
        qk_hi_made = sem("qk_hi_made")
        qk_lo_made = sem("qk_lo_made")
        v_ready = sem("v_ready")
        v_made = sem("v_made")
        qk_stored = [sem(f"qk_stored{i}") for i in range(2)]
        v_stored = sem("v_stored")

        v_flat = v_out[:, :, :, :].rearrange("p a t n -> p (a t n)").rearrange("p (w c n) -> p w c n", w=2, c=C)
        W_raw = [a[:, :, :].bitcast(F32).rearrange("p a n -> p (a n)").rearrange("p (c n) -> p c n", c=C)
                 for a in (hi_out, lo_out)] + [v_flat[:, 0], v_flat[:, 1]]
        W_scale = [1.0 / 8.0, 1.0, 1.0, 1.0]
        LN_OPS = 2 * T + 7
        LN_AT = 4

        block = ctx.enter_context(nc.Block())

        @block.sync
        def _(sp):
            sp.dma_start(xs[:, :, :], x[0].rearrange("(t p) n -> p t n", p=P)).then_inc(x_loaded, 16)
            for i, w in enumerate((Wq, Wk, Wv, Wo)):
                sp.dma_start(W_raw[i], w.rearrange("(c p) n -> p c n", p=P)).then_inc(w_loaded[i], 16)
            with nc.allow_non_contiguous_dma(reason="two vectors of 512, once"):
                sp.dma_start(bqk[:, :, 0], bq.rearrange("(c p) -> p c", p=P)).then_inc(bias_loaded, 16)
                sp.dma_start(bqk[:, :, 1], bk.rearrange("(c p) -> p c", p=P)).then_inc(bias_loaded, 16)
            sp.dma_start(bv_bc[:, :], bv.rearrange("(a n) -> a n", a=1).partition_broadcast(P)).then_inc(bias_loaded, 16)
            sp.dma_start(bo_bc[:, :], bo.rearrange("(a n) -> a n", a=1).partition_broadcast(P)).then_inc(bias_loaded, 16)

            def load_adj(t):
                after(sp, maskT_made, 2 * (t - 1))
                after(sp, mask_made, t - 1)
                sp.dma_start(adj_sb[:, t % 2, :], adj[t * P:(t + 1) * P, :]).then_inc(adj_loaded[t % 2], 16)

            load_adj(0)
            load_adj(1)

            def load_x(b):
                sp.wait_ge(h_turned, b * T)
                sp.dma_start(xs[:, :, :], x[b].rearrange("(t p) n -> p t n", p=P)).then_inc(x_loaded, 16)

            def step(b, left):
                for j in range(J):
                    sp.wait_ge(qk_hi_made, b * J + (j + 1))
                    sp.dma_start(qk_d[b, j // 2, 2 * (j % 2)], hi_out[:, j % 2, :].bitcast(F32)).then_inc(qk_stored[j % 2], 16)
                    sp.wait_ge(qk_lo_made, b * J + (j + 1))
                    sp.dma_start(qk_d[b, j // 2, 2 * (j % 2) + 1], lo_out[:, j % 2, :].bitcast(F32)).then_inc(qk_stored[j % 2], 16)
                    if masks_beside(b) and j + 2 < T:
                        load_adj(j + 2)
                if left >= 2:
                    load_x(b + 2)
                sp.wait_ge(v_made, b * T + T)
                sp.dma_start(v_d[b].rearrange("a p n -> p a n"),
                             v_out[:, :, :, :].rearrange("p a t n -> p a (t n)")).then_inc(v_stored, 16)

            load_x(1)
            batches(sp, B, step)
            for i in range(2):
                sp.wait_ge(qk_stored[i], 32 * (J // 2) * B)
            sp.wait_ge(v_stored, 16 * B)

        @block.gpsimd
        def _(pool):
            nc.gpsimd.memset(ident[:, :], 0.0).then_inc(zeroed, 1)
            pool.wait_ge(zeroed, 1)
            nc.gpsimd.affine_select(out=ident[:, :], in_=ident[:, :], compare_op=ALU.not_equal, fill=1.0, base=0,
                                    pattern=[[-1, P]], channel_multiplier=1).then_inc(ident_made, 1)

        @block.scalar
        def _(act):
            def weights_hi(weights):
                for i in weights:
                    act.wait_ge(w_loaded[i], 16)
                    nc.scalar.mul(W_hi[i][:, :, :], W_raw[i], W_scale[i]).then_inc(w_hi_made, 1)

            def sqrt(b):
                act.wait_ge(ln_steps, b * LN_OPS + 2 * T + 2)
                nc.scalar.activation(y0[:, :], rv[:, :], ACT.Sqrt).then_inc(sqrt_made, 1)

            def relu_ln(b, tiles):
                act.wait_ge(ln_steps, b * LN_OPS + LN_OPS)
                for t in tiles:
                    nc.scalar.activation(xs[:, t, :], xs[:, t, :], ACT.Relu, bias=nmr[:, t:t + 1],
                                         scale=rstd[:, t:t + 1]).then_inc(h_made, 1)

            def turned_hi(b, t):
                act.wait_ge(h_turned, b * T + (t + 1))
                nc.scalar.copy(hT_hi[:, :, t * P:(t + 1) * P],
                               tp[:, t % 2, :].rearrange("p (c n) -> p c n", c=C)).then_inc(hT_hi_made, 1)

            def step(b, left):
                for j in range(J):
                    act.wait_ge(qk_ready, b * J + (j + 1))
                    after(act, qk_stored[j % 2], b * (32 * (J // 2)) + 32 * (j // 2))
                    nc.scalar.activation(hi_out[:, j % 2, :], qk_ps[:, j % 2, :], ACT.Identity,
                                         bias=bqk[:, j // 2, j % 2:j % 2 + 1]).then_inc(qk_hi_made, 1)
                    if left and j == LN_AT:
                        sqrt(b + 1)
                    if left and j > LN_AT:
                        relu_ln(b + 1, range(T)[3 * (j - LN_AT - 1):3 * (j - LN_AT)])
                if left:
                    for t in range(T):
                        turned_hi(b + 1, t)

            sqrt(0)
            weights_hi((0, 1))
            relu_ln(0, range(T))
            for t in range(T):
                turned_hi(0, t)
            weights_hi((2, 3))
            act.wait_ge(bias_scaled, 1)
            batches(act, B, step)

        @block.vector
        def _(dve):
            def weights_lo(weights):
                for i in weights:
                    dve.wait_ge(w_hi_made, i + 1)
                    nc.vector.scalar_tensor_tensor(out=W_lo[i][:, :, :].rearrange("p c n -> p (c n)"),
                                                   in0=W_raw[i].rearrange("p c n -> p (c n)"), scalar=W_scale[i],
                                                   in1=W_hi[i][:, :, :].bitcast(F32).rearrange("p c n -> p (c n)"),
                                                   op0=ALU.mult, op1=ALU.subtract).then_inc(w_lo_made, 1)

            def row_stats(b, tiles):
                dve.wait_ge(x_loaded, b * 16 + 16)
                for t in tiles:
                    nc.vector.bn_stats(stats[:, t, :], xs[:, t, :]).then_inc(ln_steps, 1)

            def layer_norm(b):
                at = b * LN_OPS
                wait_apart(dve, ln_steps, at + T, stats_passed)
                for t in range(T):
                    nc.vector.bn_aggr(mv[:, t, :], stats[:, t, :]).then_inc(ln_steps, 1)
                dve.wait_ge(ln_steps, at + 2 * T)
                nc.vector.tensor_scalar(ve[:, :], mv[:, :, 1], EPS, None, ALU.add).then_inc(ln_steps, 1)
                dve.wait_ge(ln_steps, at + 2 * T + 1)
                nc.vector.reciprocal(rv[:, :], ve[:, :]).then_inc(ln_steps, 1)
                dve.wait_ge(sqrt_made, b + 1)
                nc.vector.tensor_tensor(t1[:, :], y0[:, :], y0[:, :], ALU.mult).then_inc(ln_steps, 1)
                dve.wait_ge(ln_steps, at + 2 * T + 3)
                nc.vector.tensor_tensor(t2[:, :], t1[:, :], ve[:, :], ALU.mult).then_inc(ln_steps, 1)
                dve.wait_ge(ln_steps, at + 2 * T + 4)
                nc.vector.tensor_scalar(t3[:, :], t2[:, :], -0.5, 1.5, ALU.mult, ALU.add).then_inc(ln_steps, 1)
                dve.wait_ge(ln_steps, at + 2 * T + 5)
                nc.vector.tensor_tensor(rstd[:, :], y0[:, :], t3[:, :], ALU.mult).then_inc(ln_steps, 1)
                dve.wait_ge(ln_steps, at + 2 * T + 6)
                nc.vector.scalar_tensor_tensor(out=nmr[:, :], in0=mv[:, :, 0], scalar=-1.0, in1=rstd[:, :],
                                               op0=ALU.mult, op1=ALU.mult).then_inc(ln_steps, 1)

            def make_masks(t):
                for h in range(2):
                    dve.wait_ge(adj_turned, 2 * t + h + 1)
                    nc.vector.tensor_scalar(maskT[:, 4 * h:4 * h + 4, t * P:(t + 1) * P],
                                            v_ps[:, h, :].rearrange("p (k n) -> p k n", k=4), -1.0, None,
                                            ALU.add).then_inc(maskT_made, 1)
                nc.vector.tensor_scalar(mask[:, t, :], adj_sb[:, t % 2, :], -1.0, BIG, ALU.add,
                                        ALU.mult).then_inc(mask_made, 1)

            def turned_lo(b, t):
                dve.wait_ge(hT_hi_made, b * T + (t + 1))
                cols = slice(t * P, (t + 1) * P)
                nc.vector.tensor_tensor(hT_lo[:, :, cols], tp[:, t % 2, :].rearrange("p (c n) -> p c n", c=C),
                                        hT_hi[:, :, cols].bitcast(F32), ALU.subtract).then_inc(hT_lo_made, 1)

            def step(b, left):
                for j in range(J):
                    dve.wait_ge(qk_hi_made, b * J + (j + 1))
                    nc.vector.scalar_tensor_tensor(out=lo_out[:, j % 2, :], in0=qk_ps[:, j % 2, :],
                                                   scalar=bqk[:, j // 2, j % 2:j % 2 + 1],
                                                   in1=hi_out[:, j % 2, :].bitcast(F32), op0=ALU.add,
                                                   op1=ALU.subtract).then_inc(qk_lo_made, 1)
                    if masks_beside(b):
                        make_masks(j)
                    if left and j in (LN_AT - 2, LN_AT - 1):
                        at = (j - LN_AT + 2) * (T // 2)
                        row_stats(b + 1, range(at, at + T // 2))
                    if left and j == LN_AT:
                        layer_norm(b + 1)
                after(dve, v_stored, b * 16)
                for t in range(T):
                    dve.wait_ge(v_ready, b * T + (t + 1))
                    nc.vector.tensor_tensor(v_out[:, :, t, :], v_ps[:, t % 2, :].rearrange("p (a n) -> p a n", a=PAIRS),
                                            bv_bc[:, :].rearrange("p (a n) -> p a n", a=PAIRS),
                                            ALU.add).then_inc(v_made, 1)
                    if left:
                        turned_lo(b + 1, t)

            row_stats(0, range(T))
            layer_norm(0)
            weights_lo((0, 1))
            for t in range(T):
                turned_lo(0, t)
            weights_lo((2, 3))
            dve.wait_ge(bias_loaded, 64)
            nc.vector.tensor_scalar(bqk[:, :, 0], bqk[:, :, 0], W_scale[0], None, ALU.mult).then_inc(bias_scaled, 1)
            dve.wait_ge(ident_made, 1)
            nc.vector.tensor_copy(identb[:, :], ident[:, :]).then_inc(identb_made, 1)
            batches(dve, B, step)

        @block.tensor
        def _(pe):
            def turn_adj(t):
                pe.wait_ge(adj_loaded[t % 2], 16 * (t // 2 + 1))
                for h in range(2):
                    after(pe, maskT_made, 2 * (t - 1) + h + 1)
                    for i in range(4):
                        kt = 4 * h + i
                        mm = pe.transpose(v_ps[:, h, i * P:(i + 1) * P], adj_sb[:, t % 2, kt * P:(kt + 1) * P], ident[:, :])
                    mm.then_inc(adj_turned, 1)

            def three_passes(out, lhs, rhs, n):
                for c in range(n):
                    for k, (l, r) in enumerate(((0, 0), (0, 1), (1, 0))):
                        mm = pe.matmul(out, lhs(l, c), rhs(r, c), start=(c == 0 and k == 0), stop=(c == n - 1 and k == 2))
                return mm

            hT = (hT_hi, hT_lo)

            def turn(b, t):
                pe.wait_ge(h_made, b * T + (t + 1))
                after(pe, hT_lo_made, b * T + (t - 1))
                for c in range(C):
                    mm = pe.transpose(tp[:, t % 2, c * P:(c + 1) * P], xs[:, t, c * P:(c + 1) * P], ident[:, :])
                mm.then_inc(h_turned, 1)

            def step(b, left):
                for j in range(J):
                    w = (W_hi[j % 2], W_lo[j % 2])
                    after(pe, qk_lo_made, b * J + (j - 1))
                    for h, cols in halves():
                        if j == 0:
                            pe.wait_ge(hT_lo_made, b * T + 4 * (h + 1))
                        mm = three_passes(qk_ps[:, j % 2, cols],
                                          lambda l, c: w[l][:, c, (j // 2) * P:(j // 2 + 1) * P],
                                          lambda r, c: hT[r][:, c, cols], C)
                    mm.then_inc(qk_ready, 1)
                    if masks_beside(b):
                        turn_adj(j)
                if masks_beside(b):
                    pe.wait_ge(w_lo_made, 4)
                    pe.wait_ge(maskT_made, 2 * T)
                for t in range(T):
                    after(pe, v_made, b * T + (t - 1))
                    mm = three_passes(v_ps[:, t % 2, :], lambda l, c: hT[l][:, c, t * P:(t + 1) * P],
                                      lambda r, c: (W_hi[2], W_lo[2])[r][:, c, :], C)
                    mm.then_inc(v_ready, 1)
                    if left:
                        turn(b + 1, t)

            pe.wait_ge(ident_made, 1)
            for t in range(T):
                turn(0, t)
            pe.wait_ge(w_lo_made, 2)
            batches(pe, B, step)


def masks_beside(b):
    return isinstance(b, int) and b == 0


def batches(eng, count, step):
    step(0, count - 1)
    with eng.Fori(1, count - 2) as b:
        step(b, 2)
    step(count - 2, 1)
    step(count - 1, 0)


def slot_order(T, kind):
    sums = [("sum",), ("ln",), ("exp_ln",)]
    norm = [("norm",), ("high",), ("low",)]

    def piece(i):
        u, at = divmod(i, 8)
        return (([("bo", u)] if at == 0 else []) + [("out", u, 2 * u + at % 2, at // 2)] +
                ([("add", u), ("sty", u)] + ([("ldx", u + 2)] if u < 2 else []) if at == 7 else []))

    if kind == "lead":
        items = [("load_v",), ("load",)]
        for hd in range(2):
            items += [("mx", j) for j in range(hd * T, hd * T + T)] + [("split", hd, i) for i in range(SPLIT_STEPS)]
        return items + [("mrow", 0), ("keep", 0), ("mrow", 1), ("keep", 1), ("rows_kept",)]
    if kind == "tail":
        pieces = [piece(i) for i in range(4 * T)]
        first, second, others = pieces[0:6], pieces[8:14], pieces[6:8] + pieces[14:]
        return ([("ldx", 0), ("ldx", 1), ("w", 0, 0), ("w", 0, 1), ("copy_o",)] + sum(first, []) + sums +
                sum(second, []) + norm + sum(others, []) + [("stored",)])
    behind, ahead, outs = kind != "first", kind != "last", kind == "outs"
    letters_of = STEPS[kind if kind in STEPS else "plain"]
    items = [("ldx", 0), ("ldx", 1)] if outs else []
    mxs = 0
    pieces = "".join(STEPS["outs"]).count("o") if kind == "after" else 0
    split = []
    for t, letters in enumerate(letters_of):
        heads = ws = 0
        for letter in letters:
            if letter == "s":
                items += [("st", t, heads), ("exp", t, heads)]
                heads += 1
                if heads == 2:
                    items += [("acc", t, hd) for hd in range(2)] if t else []
                    items += [("load",)] if t == T - 1 else []
            if letter == "w" and (t or behind):
                items.append(("w", t, ws))
                ws += 1
                if t == 0 and ws == 2:
                    items.append(("copy_o",))
            if letter == "m" and ahead:
                items.append(("mx", mxs))
                if split:
                    items += split.pop(0)
                if mxs == T - 1:
                    split = [[("split", 0, k) for k in ks] for ks in ((0, 1), (2, 3), (4, 5))]
                    split.append([("mrow", 0), ("keep", 0)])
                if mxs == 2 * T - 1:
                    items += [("split", 1, k) for k in range(SPLIT_STEPS)]
                mxs += 1
            if letter == "r" and ahead:
                items += [("mrow", 1), ("keep", 1)]
            if letter == "z" and behind:
                items += sums
            if letter == "n" and behind:
                items += norm
            if letter == "o":
                items += piece(pieces)
                pieces += 1
        if t == 0 and ahead:
            items.append(("load_v",))
    if ahead:
        items.append(("rows_kept",))
    if kind == "after":
        items.append(("stored",))
    return items


class Order:

    READ_BY = {"st": None, "mx": None, "mrow": "keep", "sum": "ln", "out": "add"}

    def __init__(self, T, kind):
        self.kind = kind
        self.items = slot_order(T, kind)
        self.count = [0] * PLACES
        self.unit = {}
        free_at = [i - PLACES for i in range(PLACES)]
        for at, item in enumerate(self.items):
            if item[0] not in self.READ_BY or self.key(item) in self.unit:
                continue
            place = min(range(PLACES), key=lambda i: free_at[i])
            assert free_at[place] < at
            self.unit[self.key(item)] = (place, self.count[place])
            self.count[place] += 1
            reader = self.READ_BY[item[0]]
            free_at[place] = at if reader is None else self.items.index((reader,) + self.key(item)[1:])

    @staticmethod
    def key(item):
        return ("out", item[1]) if item[0] in ("out", "add") else item

    def last_of(self, keys):
        last = {}
        for key in keys:
            place, number = self.unit[key]
            last[place] = number + 1
        return last


def attend_stage(nc, sh, io, scratch, keep, out):
    x = io[0]
    qk_d, v_d = scratch
    mask, maskT, Wo_hi, Wo_lo, bo_bc, _, identb = keep
    B, N, D, T, PAIRS, HD = sh.B, sh.N, sh.D, sh.T, sh.PAIRS, sh.HD
    HT = 2 * T
    OU = T // 2
    MROWS = 3
    KB_ROWS = HD + MROWS
    ADDS = 2 * (T - 1)
    NS = B * PAIRS
    with ExitStack() as ctx:
        def sb(name, shape, dt):
            return ctx.enter_context(nc.sbuf_tensor(name, shape, dt))

        def sem(name):
            return ctx.enter_context(nc.semaphore(name))

        k_hl = sb("k_hl", [P, 2, 2, N], F32R)
        q_hh = sb("q_hh", [P, 2, 2, N], F32R)
        k_h1 = sb("k_h1", [P, 2, 2, N], F32R)
        q_lm = sb("q_lm", [P, 2, 2, N], F32R)
        v_sb = sb("v_sb", [P, 2, T, P], F32)
        probs = sb("probs", [P, 2, 2, N], F32)
        acc = sb("acc", [P, 2, 2, N], F32)
        o_sb = sb("o_sb", [P, N], F32)
        rsum = sb("rsum", [P, N], F32)
        oT_hi = sb("oT_hi", [P, PAIRS, N], F32R)
        oT_lo = sb("oT_lo", [P, PAIRS, N], F32R)
        xy = sb("xy", [P, 2, 2, D], F32)
        ones = sb("ones", [P, HD], F32)
        qmax = sb("qmax", [P, 2, T], F32)
        empty = sb("empty", [P, 2, T], F32)
        rest = sb("rest", [P, 2, T], F32)
        pieces = sb("pieces", [P, 2, T, KB_ROWS + 1], BF16)

        place_ps = [ctx.enter_context(nc.psum_tensor(f"place_ps{i}", [P, N], F32)) for i in range(PLACES)]
        o_ps = ctx.enter_context(nc.psum_tensor("o_ps", [P, N], F32))

        ready = [sem(f"ready{i}") for i in range(PLACES)]
        read = [sem(f"read{i}") for i in range(PLACES)]
        qk_loaded = [[sem(f"qk_loaded{i}{hd}") for hd in range(2)] for i in range(2)]
        qk2_loaded = [sem(f"qk2_loaded{i}") for i in range(2)]
        v_loaded = [sem(f"v_loaded{i}") for i in range(2)]
        x_loaded = [sem(f"x2_loaded{i}") for i in range(2)]
        y_stored = [sem(f"y_stored{i}") for i in range(2)]
        consts = sem("consts")
        q_lm_zeroed = sem("q_lm_zeroed")
        mx_passed = sem("mx_passed")
        sp_passed = sem("sp_passed")
        m_steps = sem("m_steps")
        exp_done = sem("exp_done")
        pv_done = sem("pv_done")
        o_copied = sem("o_copied")
        added = sem("added")
        recip_ready = sem("recip_ready")
        o_normed = sem("o_normed")
        oT_hi_made = sem("oT_hi_made")
        oT_lo_made = sem("oT_lo_made")
        xbo_made = sem("xbo_made")

        block = ctx.enter_context(nc.Block())

        orders = {kind: Order(T, kind) for kind in ("lead", "first", "plain", "outs", "after", "last", "tail")}
        ALONE = {-1: "lead", 0: "first", 1: "plain", NS - 1: "last", NS: "tail"}
        BODY = ["outs", "after"] + ["plain"] * (PAIRS - 2)

        class Slot:
            def __init__(self, n, p, half, b):
                self.n, self.p, self.half, self.b = n, p, half, b
                self.par, self.nxt = p % 2, (p + 1) % 2
                is_int = isinstance(n, int)
                self.kind = ALONE.get(n, BODY[p]) if is_int else BODY[p]
                self.order = orders[self.kind]
                if is_int:
                    before = [ALONE.get(m, BODY[m % PAIRS]) for m in range(-1, n)]
                    self.before = [sum(orders[k].count[i] for k in before) for i in range(PLACES)]
                else:
                    before = ["lead"] + [ALONE.get(m, BODY[m]) for m in range(PAIRS)] + BODY[:p]
                    self.before = [b * sum(orders[k].count[i] for k in BODY) + sum(orders[k].count[i] for k in before)
                                   for i in range(PLACES)]

            def place(self, item):
                return self.order.unit[Order.key(item)][0]

            def count(self, item):
                place, number = self.order.unit[Order.key(item)]
                return self.before[place] + (number + 1)

            def wait_free(self, eng, item):
                place, number = self.order.unit[Order.key(item)]
                if self.kind != "lead" or number:
                    eng.wait_ge(read[place], self.before[place] + number)

            def wait_made(self, eng, item):
                eng.wait_ge(ready[self.place(item)], self.count(item))

            def wait_read(self, eng, item):
                eng.wait_ge(read[self.place(item)], self.count(item))

        def every_slot(eng, slot):
            for n in range(-1, PAIRS):
                slot(Slot(n, n % PAIRS, n // 2, -1))
            with eng.Fori(0, B - 2) as b:
                for p in range(PAIRS):
                    slot(Slot(b * PAIRS + (PAIRS + p), p, b * (PAIRS // 2) + (PAIRS + p) // 2, b))
            for n in range(NS - PAIRS, NS + 1):
                slot(Slot(n, n % PAIRS, n // 2, n // PAIRS - 1))

        @block.sync
        def _(sp):
            def load_qk(b, pair, par):
                QHI, QLO, KHI, KLO = range(4)
                lo, hi = slice(0, HD), slice(HD, P)
                for hd in range(2):
                    for dst, rows, i in ((q_hh, lo, QHI), (k_hl, lo, KHI), (q_hh, hi, QHI), (k_hl, hi, KLO)):
                        sp.dma_start(dst[rows, par, hd].bitcast(F32),
                                     qk_d[b, pair, i, hd * HD:(hd + 1) * HD]).then_inc(qk_loaded[par][hd], 16)
                for dst, i in ((k_h1, KHI), (q_lm, QLO)):
                    sp.dma_start(dst[lo, par].bitcast(F32),
                                 qk_d[b, pair, i].rearrange("(h p) n -> p h n", h=2)).then_inc(qk2_loaded[par], 16)

            def rows_of(a, b, u):
                return a[b, 2 * u * P:2 * (u + 1) * P, :].rearrange("(t p) n -> p t n", p=P)

            load_qk(0, 0, 0)

            def slot(s):
                n, p, b, order = s.n, s.p, s.b, s.order
                for item in order.items:
                    if item[0] == "load" and not (isinstance(n, int) and n + 2 >= NS):
                        for place, number in order.last_of(k for k in order.unit if k[0] == "st").items():
                            wait_apart(sp, ready[place], s.before[place] + number, sp_passed)
                        load_qk(batch_of(n, p, b, 2), (p + 2) % PAIRS, s.par)
                    if item[0] == "load_v":
                        if s.kind not in ("lead", "first"):
                            wait_apart(sp, pv_done, n * T, sp_passed)
                        sp.dma_start(v_sb[:, s.nxt].rearrange("p t n -> p (t n)"),
                                     v_d[batch_of(n, p, b, 1), (p + 1) % PAIRS]).then_inc(v_loaded[s.nxt], 16)
                    if item[0] == "ldx":
                        u = item[1]
                        if u >= 2:
                            wait_apart(sp, y_stored[u % 2], b * (16 * OU // 2) + 16 * (u // 2), sp_passed)
                        sp.dma_start(xy[:, u % 2], rows_of(x, b, u)).then_inc(x_loaded[u % 2], 16)
                    if item[0] == "sty":
                        wait_apart(sp, read[s.place(("out", item[1]))], s.count(("out", item[1])), sp_passed)
                        sp.dma_start(rows_of(out, b, item[1]), xy[:, item[1] % 2]).then_inc(y_stored[item[1] % 2], 16)
                    if item[0] == "stored":
                        for i in range(2):
                            wait_apart(sp, y_stored[i], (b + 1) * (16 * OU // 2), sp_passed)

            def batch_of(n, p, b, more):
                if isinstance(n, int):
                    return (n + more) // PAIRS
                return b + (PAIRS + p + more) // PAIRS

            every_slot(sp, slot)

        @block.gpsimd
        def _(pool):
            nc.gpsimd.memset(pieces[:, :, :, :], 0.0).then_inc(consts, 1)
            nc.gpsimd.memset(ones[:, :], 1.0).then_inc(consts, 1)
            pool.wait_ge(consts, 2)
            nc.gpsimd.memset(k_h1[HD:P, :, :, :].bitcast(F32), 1.0).then_inc(consts, 1)
            nc.gpsimd.memset(q_lm[HD:P, :, :, :].bitcast(F32), 0.0).then_inc(q_lm_zeroed, 1)
            pool.wait_ge(q_lm_zeroed, 1)

            def accumulate(s, t, hd):
                pool.wait_ge(exp_done, s.n * HT + (2 * t + hd + 1))
                if t == 1:
                    before = probs[:, 0, hd, :]
                else:
                    pool.wait_ge(added, s.n * ADDS + (2 * (t - 2) + hd + 1))
                    before = acc[:, s.par, hd, :]
                nc.gpsimd.tensor_tensor(acc[:, s.par, hd, :], before, probs[:, t % 2, hd, :], ALU.add).then_inc(added, 1)

            def norm(n):
                pool.wait_ge(recip_ready, n + 1)
                nc.gpsimd.tensor_tensor(o_sb[:, :], o_sb[:, :], rsum[:, :], ALU.mult).then_inc(o_normed, 1)

            def low_part(n, pair):
                pool.wait_ge(oT_hi_made, n + 1)
                nc.gpsimd.tensor_tensor(oT_lo[:, pair, :], o_sb[:, :], oT_hi[:, pair, :].bitcast(F32),
                                        ALU.subtract).then_inc(oT_lo_made, 1)

            def add_bo(b, u):
                pool.wait_ge(x_loaded[u % 2], b * (16 * OU // 2) + 16 * (u // 2 + 1))
                for i in range(2):
                    nc.gpsimd.tensor_tensor(xy[:, u % 2, i, :], xy[:, u % 2, i, :], bo_bc[:, :], ALU.add).then_inc(xbo_made, 1)

            def slot(s):
                for item in s.order.items:
                    if item[0] == "acc":
                        accumulate(s, item[1], item[2])
                    if item[0] == "norm":
                        norm(s.n - 1)
                    if item[0] == "low":
                        low_part(s.n - 1, (s.p - 1) % PAIRS)
                    if item[0] == "bo":
                        add_bo(s.b, item[1])

            every_slot(pool, slot)

        @block.scalar
        def _(act):
            def keep_mrows(s, hd):
                s.wait_made(act, ("mrow", hd))
                place = s.place(("mrow", hd))
                nc.scalar.copy(q_lm[HD:KB_ROWS, s.nxt, hd, :], place_ps[place][HD:KB_ROWS, :]).then_inc(read[place], 1)

            def slot(s):
                n = s.n
                for item in s.order.items:
                    if item[0] == "exp":
                        _, t, hd = item
                        s.wait_read(act, ("st", t, hd))
                        pr = probs[:, t % 2, hd, :]
                        nc.scalar.activation(pr, pr, ACT.Exp).then_inc(exp_done, 1)
                    if item[0] == "copy_o":
                        act.wait_ge(pv_done, n * T)
                        nc.scalar.copy(o_sb[:, :], o_ps[:, :]).then_inc(o_copied, 1)
                    if item[0] == "ln":
                        s.wait_made(act, ("sum",))
                        place = s.place(("sum",))
                        nc.scalar.activation(rsum[:, :], place_ps[place][:, :], ACT.Ln).then_inc(read[place], 1)
                    if item[0] == "exp_ln":
                        s.wait_read(act, ("sum",))
                        nc.scalar.activation(rsum[:, :], rsum[:, :], ACT.Exp, scale=-1.0).then_inc(recip_ready, 1)
                    if item[0] == "high":
                        act.wait_ge(o_normed, n)
                        nc.scalar.copy(oT_hi[:, (s.p - 1) % PAIRS, :], o_sb[:, :]).then_inc(oT_hi_made, 1)
                    if item[0] == "keep":
                        keep_mrows(s, item[1])

            act.wait_ge(q_lm_zeroed, 1)
            every_slot(act, slot)

        @block.vector
        def _(dve):
            def mask_scores(s, t, hd):
                s.wait_made(dve, ("st", t, hd))
                after(dve, pv_done, s.n * T + (t - 1))
                last = max(t - 2, 1) if t >= 2 else T + t - 2
                after(dve, added, s.n * ADDS + (2 * (last - 1) + hd + 1 - (ADDS if t < 2 else 0)))
                place = s.place(("st", t, hd))
                nc.vector.scalar_tensor_tensor(out=probs[:, t % 2, hd, :], in0=maskT[:, t, :], scalar=NEG,
                                               in1=place_ps[place][:, :], op0=ALU.mult, op1=ALU.add).then_inc(read[place], 1)

            def take_max(s, j):
                place = s.place(("mx", j))
                wait_apart(dve, ready[place], s.count(("mx", j)), mx_passed)
                ps = place_ps[place][:, :]
                nc.vector.tensor_tensor_reduce(ps, ps, mask[:, j % T, :], 1.0, -3.0e38, ALU.add, ALU.max,
                                               qmax[:, j // T, j % T:j % T + 1]).then_inc(read[place], 1)

            def split_max(s, hd, i):
                piece = [pieces[:, hd, :, HD + i] for i in range(MROWS)]
                q, e, r = qmax[:, hd, :], empty[:, hd, :], rest[:, hd, :]
                if i == 0:
                    for place, number in s.order.last_of([("mx", j) for j in range(hd * T, hd * T + T)]).items():
                        dve.wait_ge(read[place], s.before[place] + number)
                    op = nc.vector.tensor_scalar(e, q, -BIG / 2, BIG - NEG, ALU.is_lt, ALU.mult)
                else:
                    dve.wait_ge(m_steps, (s.n + 1) * (2 * SPLIT_STEPS) + (SPLIT_STEPS * hd + i))
                if i == 1:
                    op = nc.vector.tensor_tensor(q, q, e, ALU.add)
                if i == 2:
                    op = nc.vector.tensor_scalar(piece[0], q, -1.0, None, ALU.mult)
                if i == 3:
                    op = nc.vector.scalar_tensor_tensor(out=r, in0=q, scalar=-1.0, in1=piece[0], op0=ALU.mult, op1=ALU.subtract)
                if i == 4:
                    op = nc.vector.tensor_copy(piece[1], r)
                if i == 5:
                    op = nc.vector.tensor_tensor(piece[2], r, piece[1], ALU.subtract)
                op.then_inc(m_steps, 1)

            def add_out(s, u):
                s.wait_made(dve, ("out", u))
                dve.wait_ge(xbo_made, s.b * T + (2 * u + 2))
                place = s.place(("out", u))
                tiles = xy[:, u % 2].rearrange("p t n -> p (t n)")
                nc.vector.tensor_tensor(tiles, place_ps[place][:, :], tiles, ALU.add).then_inc(read[place], 1)

            def slot(s):
                for item in s.order.items:
                    if item[0] == "st":
                        mask_scores(s, item[1], item[2])
                    if item[0] == "mx":
                        take_max(s, item[1])
                    if item[0] == "split":
                        split_max(s, item[1], item[2])
                    if item[0] == "add":
                        add_out(s, item[1])

            dve.wait_ge(consts, 1)
            every_slot(dve, slot)

        @block.tensor
        def _(pe):
            def query_scores(s, j):
                hd, qt = j // T, j % T
                if qt == 0:
                    pe.wait_ge(qk_loaded[s.nxt][hd], (s.half + s.par + 1) * 64)
                s.wait_free(pe, ("mx", j))
                place = s.place(("mx", j))
                for h, cols in halves():
                    mm = pe.matmul(place_ps[place][:, cols], q_hh[:, s.nxt, hd, qt * P:(qt + 1) * P],
                                   k_hl[:, s.nxt, hd, cols], start=True, stop=True)
                mm.then_inc(ready[place], 1)

            def max_rows(s, hd):
                s.wait_free(pe, ("mrow", hd))
                pe.wait_ge(m_steps, (s.n + 1) * (2 * SPLIT_STEPS) + SPLIT_STEPS * (hd + 1))
                place = s.place(("mrow", hd))
                for qt in range(T):
                    mm = pe.matmul(place_ps[place][0:KB_ROWS, qt * P:(qt + 1) * P], pieces[:, hd, qt, 0:KB_ROWS],
                                   identb[:, :], start=True, stop=True)
                mm.then_inc(ready[place], 1)

            def key_scores(s, t, hd):
                par = s.par
                if t == 0 and hd == 0:
                    pe.wait_ge(qk2_loaded[par], (s.half + 1) * 32)
                s.wait_free(pe, ("st", t, hd))
                keys = slice(t * P, (t + 1) * P)
                place = s.place(("st", t, hd))
                for h, cols in halves():
                    pe.matmul(place_ps[place][:, cols], k_hl[:, par, hd, keys], q_hh[:, par, hd, cols], start=True, stop=False)
                for h, cols in halves():
                    mm = pe.matmul(place_ps[place][:, cols], k_h1[:, par, hd, keys], q_lm[:, par, hd, cols],
                                   start=False, stop=True)
                mm.then_inc(ready[place], 1)

            def weigh(n, t, h, par, loads):
                if t == 0 and h == 0:
                    pe.wait_ge(v_loaded[par], loads * 16)
                    after(pe, o_copied, n)
                if h == 0:
                    pe.wait_ge(exp_done, n * HT + (2 * t + 2))
                cols = slice(h * BANK, (h + 1) * BANK)
                for hd in range(2):
                    rows = slice(hd * HD, (hd + 1) * HD)
                    mm = pe.matmul(o_ps[rows, cols], v_sb[:, par, t, rows], probs[:, t % 2, hd, cols],
                                   start=(t == 0), stop=(t == T - 1))
                if h == 1:
                    mm.then_inc(pv_done, 1)

            def sums(s):
                s.wait_free(pe, ("sum",))
                pe.wait_ge(added, s.n * ADDS)
                place = s.place(("sum",))
                for h, cols in halves():
                    for hd in range(2):
                        rows = slice(hd * HD, (hd + 1) * HD)
                        mm = pe.matmul(place_ps[place][rows, cols], ones[:, :], acc[:, s.nxt, hd, cols], start=True, stop=True)
                mm.then_inc(ready[place], 1)

            def project_out(s, u, i, c):
                toks = slice(i * P, (i + 1) * P)
                place = s.place(("out", u))
                if i == 0 and c in (0, PAIRS - 1):
                    pe.wait_ge(oT_lo_made, s.b * PAIRS + (PAIRS - 1 if c == 0 else PAIRS))
                if i == 2 * u and c == 0:
                    s.wait_free(pe, ("out", u))
                for k, (l, r) in enumerate(((oT_hi, Wo_hi), (oT_hi, Wo_lo), (oT_lo, Wo_hi))):
                    mm = pe.matmul(place_ps[place][:, (i % 2) * BANK:(i % 2 + 1) * BANK], l[:, c, toks], r[:, c, :],
                                   start=(c == 0 and k == 0), stop=(c == PAIRS - 1 and k == 2))
                if i == 2 * u + 1 and c == PAIRS - 1:
                    mm.then_inc(ready[place], 1)

            def slot(s):
                for item in s.order.items:
                    if item[0] == "st":
                        key_scores(s, item[1], item[2])
                    if item[0] == "mx":
                        query_scores(s, item[1])
                    if item[0] == "w":
                        _, t, h = item
                        if t == 0:
                            weigh(s.n - 1, T - 1, h, s.nxt, s.half + s.par)
                        else:
                            weigh(s.n, t - 1, h, s.par, s.half + 1)
                    if item[0] == "sum":
                        sums(s)
                    if item[0] == "mrow":
                        max_rows(s, item[1])
                    if item[0] == "rows_kept":
                        for hd in range(2):
                            s.wait_read(pe, ("mrow", hd))
                    if item[0] == "out":
                        project_out(s, item[1], item[2], item[3])

            pe.wait_ge(consts, 3)
            every_slot(pe, slot)


def graph_attention_kernel(nc, x, adj, Wq, bq, Wk, bk, Wv, bv, Wo, bo, out):
    sh = Shapes(x, heads=8)
    with ExitStack() as ctx:
        def sb(name, shape, dt):
            return ctx.enter_context(nc.sbuf_tensor(name, shape, dt))

        keep = (
            sb("mask", [P, sh.T, sh.N], BF16),
            sb("maskT", [P, sh.T, sh.N], BF16),
            sb("Wo_hi", [P, sh.C, sh.D], F32R),
            sb("Wo_lo", [P, sh.C, sh.D], F32R),
            sb("bo_bc", [P, sh.D], F32),
            sb("ident", [P, P], F32),
            sb("identb", [P, P], BF16),
        )
        qk_d = nc.dram_tensor("qk_scratch", [sh.B, sh.PAIRS, 4, P, sh.N], F32).ap()
        v_d = nc.dram_tensor("v_scratch", [sh.B, sh.PAIRS, P, sh.T * P], F32).ap()
        io = (x, adj, Wq, bq, Wk, bk, Wv, bv, Wo, bo)
        project_stage(nc, sh, ctx, io, (qk_d, v_d), keep)
        attend_stage(nc, sh, io, (qk_d, v_d), keep, out)


_INS = ["x", "adj"] + [f"L0_gnn_{n}" for n in ("Wq", "bq", "Wk", "bk", "Wv", "bv", "Wo", "bo")]


def kernel(**inputs):
    import numpy as _np
    import concourse.bacc as _bacc
    from concourse import mybir as _mybir
    from concourse.bass_utils import run_bass_kernel_spmd as _run

    nc = _bacc.Bacc("TRN2", target_bir_lowering=False, num_devices=1)
    arrays, args = {}, []
    for name in _INS:
        a = _np.ascontiguousarray(inputs[name])
        arrays[f"in_{name}"] = a
        args.append(nc.dram_tensor(f"in_{name}", a.shape, _mybir.dt.from_np(a.dtype), kind="ExternalInput").ap())
    out = nc.dram_tensor("out_0", arrays["in_x"].shape, _mybir.dt.float32, kind="ExternalOutput").ap()
    graph_attention_kernel(nc, *args, out)
    r = _run(nc, [arrays], core_ids=[0])
    return r.results[0]["out_0"]
```
